# Optimizing a Trainium2 kernel written in Bass

```python
import numpy as np
import jax
import jax.numpy as jnp

def _softmax(x, axis=-1):
    return jax.nn.softmax(x, axis=axis)
def _gelu(x):
    return jax.nn.gelu(x, approximate=True)
def _silu(x):
    return jax.nn.silu(x)
def _sigmoid(x):
    return jax.nn.sigmoid(x)
def _layernorm(x, axis=-1, eps=1e-5):
    m = jnp.mean(x, axis=axis, keepdims=True)
    v = jnp.var(x, axis=axis, keepdims=True)
    return (x - m) / jnp.sqrt(v + eps)
def _scatter_add(tgt, idx, src, axis=0):
    return tgt.at[idx].add(src)
def _segment_sum(src, seg, n):
    return jax.ops.segment_sum(src, seg, n)

kernel_name = 'mk_conv_seq_d2_conv_nchw256_d025b5'

def setup_inputs(seed: int = 0):
    np.random.seed(seed)
    _w = jnp.asarray
    def _rec_inputs():
        import jax
        import jax.numpy as jnp
        _gk = jax.random.key(seed)
        x = -0.0005207 + 1.001 * jax.random.normal(jax.random.fold_in(_gk, 1), (2, 256, 64, 64), jnp.float32)
        return x
    x = _rec_inputs()
    def _L0_conv_setup():
        import jax, jax.numpy as jnp
        import numpy as np
        import math
        NUM_HEADS = 8

        def _conv1x1(x, W, b):
            return jnp.einsum('bchw,oc->bohw', x, W) + b[None, :, None, None]
        key = jax.random.key(seed)
        ks = jax.random.split(key, 12)
        B, C, H, W = (2, 256, 64, 64)
        s = 1.0 / math.sqrt(C)
        x = jax.random.normal(ks[0], (B, C, H, W), dtype=jnp.float32)
        mask = jax.random.uniform(ks[1], (B, 1, 32, 32), dtype=jnp.float32)
        Wq = jax.random.normal(ks[2], (C, C), dtype=jnp.float32) * s
        bq = jax.random.normal(ks[3], (C,), dtype=jnp.float32) * 0.01
        Wk = jax.random.normal(ks[4], (C, C), dtype=jnp.float32) * s
        bk = jax.random.normal(ks[5], (C,), dtype=jnp.float32) * 0.01
        Wv = jax.random.normal(ks[6], (C, C), dtype=jnp.float32) * s
        bv = jax.random.normal(ks[7], (C,), dtype=jnp.float32) * 0.01
        Wf = jax.random.normal(ks[8], (C, 2 * C), dtype=jnp.float32) * (1.0 / math.sqrt(2 * C))
        bf = jax.random.normal(ks[9], (C,), dtype=jnp.float32) * 0.01
        return {'x': x, 'mask': mask, 'Wq': Wq, 'bq': bq, 'Wk': Wk, 'bk': bk, 'Wv': Wv, 'bv': bv, 'Wf': Wf, 'bf': bf}
    _L0_conv_all = _L0_conv_setup()
    _L0_conv_in = {k: v for k, v in _L0_conv_all.items() if k in ('mask', 'Wq', 'bq', 'Wk', 'bk', 'Wv', 'bv', 'Wf', 'bf', )}
    del _L0_conv_all

    def _L1_conv_setup():
        import jax, jax.numpy as jnp
        import numpy as np
        C = 256
        EPS = 1e-05

        def dwconv3x3(x, w):
            return jax.lax.conv_general_dilated(x, w, window_strides=(1, 1), padding=((1, 1), (1, 1)), dimension_numbers=('NCHW', 'OIHW', 'NCHW'), feature_group_count=x.shape[1])

        def bn(x, gamma, beta, mean, var):
            inv = gamma * jax.lax.rsqrt(var + EPS)
            return x * inv[:, None, None] + (beta - mean * inv)[:, None, None]
        key = jax.random.key(seed)
        ks = jax.random.split(key, 8)
        B, H, W = (32, 64, 64)
        inp = {'x': jax.random.normal(ks[0], (B, C, H, W), jnp.float32), 'edge_w': jax.random.normal(ks[1], (C, 1, 3, 3), jnp.float32) * 0.1, 'edge_gamma': jnp.ones((C,), jnp.float32), 'edge_beta': jnp.zeros((C,), jnp.float32), 'edge_mean': jnp.zeros((C,), jnp.float32), 'edge_var': jnp.ones((C,), jnp.float32), 'fc1_w': jax.random.normal(ks[2], (C // 16, C), jnp.float32) * 0.05, 'fc2_w': jax.random.normal(ks[3], (C, C // 16), jnp.float32) * 0.05, 'fusion_w': jax.random.normal(ks[4], (C, 2 * C), jnp.float32) * 0.05, 'fusion_b': jnp.zeros((C,), jnp.float32), 'bn1_gamma': jnp.ones((C,), jnp.float32), 'bn1_beta': jnp.zeros((C,), jnp.float32), 'bn1_mean': jnp.zeros((C,), jnp.float32), 'bn1_var': jnp.ones((C,), jnp.float32), 'deform_w': jax.random.normal(ks[5], (C, 1, 3, 3), jnp.float32) * 0.1, 'balance_w': jax.random.normal(ks[6], (C, C), jnp.float32) * 0.05, 'balance_b': jnp.zeros((C,), jnp.float32), 'bn2_gamma': jnp.ones((C,), jnp.float32), 'bn2_beta': jnp.zeros((C,), jnp.float32), 'bn2_mean': jnp.zeros((C,), jnp.float32), 'bn2_var': jnp.ones((C,), jnp.float32)}
        return inp
    _L1_conv_all = _L1_conv_setup()
    _L1_conv_in = {k: v for k, v in _L1_conv_all.items() if k in ('edge_w', 'edge_gamma', 'edge_beta', 'edge_mean', 'edge_var', 'fc1_w', 'fc2_w', 'fusion_w', 'fusion_b', 'bn1_gamma', 'bn1_beta', 'bn1_mean', 'bn1_var', 'deform_w', 'balance_w', 'balance_b', 'bn2_gamma', 'bn2_beta', 'bn2_mean', 'bn2_var', )}
    del _L1_conv_all

    return {
        "x": x,
        "L0_conv_mask": _L0_conv_in["mask"],
        "L0_conv_Wq": _L0_conv_in["Wq"],
        "L0_conv_bq": _L0_conv_in["bq"],
        "L0_conv_Wk": _L0_conv_in["Wk"],
        "L0_conv_bk": _L0_conv_in["bk"],
        "L0_conv_Wv": _L0_conv_in["Wv"],
        "L0_conv_bv": _L0_conv_in["bv"],
        "L0_conv_Wf": _L0_conv_in["Wf"],
        "L0_conv_bf": _L0_conv_in["bf"],
        "L1_conv_edge_w": _L1_conv_in["edge_w"],
        "L1_conv_edge_gamma": _L1_conv_in["edge_gamma"],
        "L1_conv_edge_beta": _L1_conv_in["edge_beta"],
        "L1_conv_edge_mean": _L1_conv_in["edge_mean"],
        "L1_conv_edge_var": _L1_conv_in["edge_var"],
        "L1_conv_fc1_w": _L1_conv_in["fc1_w"],
        "L1_conv_fc2_w": _L1_conv_in["fc2_w"],
        "L1_conv_fusion_w": _L1_conv_in["fusion_w"],
        "L1_conv_fusion_b": _L1_conv_in["fusion_b"],
        "L1_conv_bn1_gamma": _L1_conv_in["bn1_gamma"],
        "L1_conv_bn1_beta": _L1_conv_in["bn1_beta"],
        "L1_conv_bn1_mean": _L1_conv_in["bn1_mean"],
        "L1_conv_bn1_var": _L1_conv_in["bn1_var"],
        "L1_conv_deform_w": _L1_conv_in["deform_w"],
        "L1_conv_balance_w": _L1_conv_in["balance_w"],
        "L1_conv_balance_b": _L1_conv_in["balance_b"],
        "L1_conv_bn2_gamma": _L1_conv_in["bn2_gamma"],
        "L1_conv_bn2_beta": _L1_conv_in["bn2_beta"],
        "L1_conv_bn2_mean": _L1_conv_in["bn2_mean"],
        "L1_conv_bn2_var": _L1_conv_in["bn2_var"],
    }

def reference(x, L0_conv_mask, L0_conv_Wq, L0_conv_bq, L0_conv_Wk, L0_conv_bk, L0_conv_Wv, L0_conv_bv, L0_conv_Wf, L0_conv_bf, L1_conv_edge_w, L1_conv_edge_gamma, L1_conv_edge_beta, L1_conv_edge_mean, L1_conv_edge_var, L1_conv_fc1_w, L1_conv_fc2_w, L1_conv_fusion_w, L1_conv_fusion_b, L1_conv_bn1_gamma, L1_conv_bn1_beta, L1_conv_bn1_mean, L1_conv_bn1_var, L1_conv_deform_w, L1_conv_balance_w, L1_conv_balance_b, L1_conv_bn2_gamma, L1_conv_bn2_beta, L1_conv_bn2_mean, L1_conv_bn2_var):
    import jax
    import jax.numpy as jnp
    def _L0_conv_ref(x, mask, Wq, bq, Wk, bk, Wv, bv, Wf, bf):
        import jax, jax.numpy as jnp
        import numpy as np
        import math
        NUM_HEADS = 8

        def _conv1x1(x, W, b):
            return jnp.einsum('bchw,oc->bohw', x, W) + b[None, :, None, None]
        B, C, H, W = x.shape
        num = H * W
        hd = C // NUM_HEADS
        m = jax.image.resize(mask, (B, 1, H, W), method='bilinear')

        def proj(Wp, bp):
            p = _conv1x1(x, Wp, bp)
            return p.reshape(B * NUM_HEADS, hd, num).transpose(0, 2, 1)
        q = proj(Wq, bq) / math.sqrt(hd)
        k = proj(Wk, bk)
        v = proj(Wv, bv)
        attn = jax.nn.softmax(jnp.einsum('bnd,bmd->bnm', q, k), axis=-1)
        fuse = jnp.einsum('bnm,bmd->bnd', attn, v)
        fuse = fuse.transpose(0, 2, 1).reshape(B, C, H, W)
        hybrid = _conv1x1(jnp.concatenate([x, fuse], axis=1), Wf, bf)
        return hybrid * m + x * (1.0 - m)

    def _L1_conv_ref(x, edge_w, edge_gamma, edge_beta, edge_mean, edge_var, fc1_w, fc2_w, fusion_w, fusion_b, bn1_gamma, bn1_beta, bn1_mean, bn1_var, deform_w, balance_w, balance_b, bn2_gamma, bn2_beta, bn2_mean, bn2_var):
        import jax, jax.numpy as jnp
        import numpy as np
        C = 256
        EPS = 1e-05

        def dwconv3x3(x, w):
            return jax.lax.conv_general_dilated(x, w, window_strides=(1, 1), padding=((1, 1), (1, 1)), dimension_numbers=('NCHW', 'OIHW', 'NCHW'), feature_group_count=x.shape[1])

        def bn(x, gamma, beta, mean, var):
            inv = gamma * jax.lax.rsqrt(var + EPS)
            return x * inv[:, None, None] + (beta - mean * inv)[:, None, None]
        edge = jax.nn.relu(bn(dwconv3x3(x, edge_w), edge_gamma, edge_beta, edge_mean, edge_var))
        avg = jnp.mean(x, axis=(2, 3))
        att = jax.nn.relu(avg @ fc1_w.T)
        att = jax.nn.sigmoid(att @ fc2_w.T)
        enhanced = x * att[:, :, None, None]
        fused = jnp.concatenate([enhanced, edge], axis=1)
        out = jnp.einsum('bchw,oc->bohw', fused, fusion_w) + fusion_b[None, :, None, None]
        out = bn(out, bn1_gamma, bn1_beta, bn1_mean, bn1_var)
        out = dwconv3x3(out, deform_w)
        out = jnp.einsum('bchw,oc->bohw', out, balance_w) + balance_b[None, :, None, None]
        out = bn(out, bn2_gamma, bn2_beta, bn2_mean, bn2_var)
        return out * x

    def _gn(v, G=32, eps=1e-5):
        B_, C_, H_, W_ = v.shape
        g = v.reshape(B_, G, C_ // G, H_, W_)
        m = jnp.mean(g, axis=(2, 3, 4), keepdims=True)
        s = jnp.var(g, axis=(2, 3, 4), keepdims=True)
        return ((g - m) / jnp.sqrt(s + eps)).reshape(v.shape)

    def _ln_c(v, eps=1e-6):
        m = jnp.mean(v, axis=1, keepdims=True)
        s = jnp.var(v, axis=1, keepdims=True)
        return (v - m) / jnp.sqrt(s + eps)

    def _ln_t(v, eps=1e-5):
        m = jnp.mean(v, axis=-1, keepdims=True)
        s = jnp.var(v, axis=-1, keepdims=True)
        return (v - m) / jnp.sqrt(s + eps)

    def _to_tokens(v):
        B_, C_, H_, W_ = v.shape
        return v.reshape(B_, C_, H_ * W_).transpose(0, 2, 1)
    def _from_tokens(t, like):
        B_, C_, H_, W_ = like.shape
        return t.transpose(0, 2, 1).reshape(B_, C_, H_, W_)

    x = _L0_conv_ref(x, L0_conv_mask, L0_conv_Wq, L0_conv_bq, L0_conv_Wk, L0_conv_bk, L0_conv_Wv, L0_conv_bv, L0_conv_Wf, L0_conv_bf)
    x = _L1_conv_ref(x, L1_conv_edge_w, L1_conv_edge_gamma, L1_conv_edge_beta, L1_conv_edge_mean, L1_conv_edge_var, L1_conv_fc1_w, L1_conv_fc2_w, L1_conv_fusion_w, L1_conv_fusion_b, L1_conv_bn1_gamma, L1_conv_bn1_beta, L1_conv_bn1_mean, L1_conv_bn1_var, L1_conv_deform_w, L1_conv_balance_w, L1_conv_balance_b, L1_conv_bn2_gamma, L1_conv_bn2_beta, L1_conv_bn2_mean, L1_conv_bn2_var)
    return x


_drawn_inputs = setup_inputs


def setup_inputs(seed=0):
    import zlib

    import numpy as np

    out = dict(_drawn_inputs(seed))
    spreads = {'L1_conv_edge_gamma': (1.0, 0.2),
     'L1_conv_edge_beta': (0.0, 0.1),
     'L1_conv_edge_mean': (0.0, 0.1),
     'L1_conv_edge_var': (1.0, 0.6),
     'L1_conv_fusion_b': (0.0, 0.1),
     'L1_conv_bn1_gamma': (1.0, 0.2),
     'L1_conv_bn1_beta': (0.0, 0.1),
     'L1_conv_bn1_mean': (0.0, 0.1),
     'L1_conv_bn1_var': (1.0, 0.2),
     'L1_conv_balance_b': (0.0, 0.1),
     'L1_conv_bn2_gamma': (1.0, 0.2),
     'L1_conv_bn2_beta': (0.0, 0.1),
     'L1_conv_bn2_mean': (0.0, 0.1),
     'L1_conv_bn2_var': (1.0, 0.2)}
    factors = {'L0_conv_bq': 64.0,
     'L0_conv_bk': 64.0,
     'L0_conv_bv': 8.0,
     'L0_conv_bf': 6.49,
     'L1_conv_fc1_w': 8.0,
     'L1_conv_fc2_w': 8.0}
    for name, (base, spread) in spreads.items():
        noise = np.random.default_rng([zlib.crc32(name.encode()), seed]).standard_normal(out[name].shape)
        drawn = base * np.exp(spread * noise) if base else spread * noise
        out[name] = jnp.asarray(drawn.astype(out[name].dtype))
    for name, factor in factors.items():
        out[name] = (out[name] * factor).astype(out[name].dtype)
    return out
```

```python
from contextlib import ExitStack

import concourse.bass as bass
from concourse import mybir

F32 = mybir.dt.float32
F32R = mybir.dt.float32r
ALU = mybir.AluOpType
ACT = mybir.ActivationFunctionType
AX = mybir.AxisListType

P = 128
B, C, HH, WW = 2, 256, 64, 64
N = HH * WW
CT = C // P
HEADS = 8
HD = C // HEADS
QS = float(HD) ** -0.5
CH = 512
NCH = N // CH
MT = N // P
PAIRS = B * HEADS // 2
UNITS = PAIRS * NCH
ROWS = CH // WW
PW = WW + 2
PR = HH + 2
SPLIT = 3 * HD
NSUB = CH // P
MB = N // CH
MAXMM = 2 * NSUB * MB
RING = 4
EPS = 1e-5
HID = C // 16
TAPS = 9

VEC = ["bq", "bk", "bf", "edge_gamma", "edge_beta", "edge_mean", "edge_var", "fusion_b",
       "bn1_gamma", "bn1_beta", "bn1_mean", "bn1_var", "balance_b",
       "bn2_gamma", "bn2_beta", "bn2_mean", "bn2_var"]
NVEC = len(VEC)
NORMS = [("edge", None), ("bn1", "fusion_b"), ("bn2", "balance_b")]
WEIGHTS = [("wq", CT, CT), ("wk", CT, CT), ("wv", CT, CT), ("wf", CT, 2 * CT), ("fu", CT, 2 * CT), ("ba", CT, CT)]


def setup_phase(nc, dram, keep):
    blocks = [(w, ot, kt) for w, ots, kts in WEIGHTS for ot in range(ots) for kt in range(kts)]
    with ExitStack() as ctx:
        sb = lambda name, shape, dt=F32: ctx.enter_context(nc.sbuf_tensor(name, shape, dt))
        sem = lambda name: ctx.enter_context(nc.semaphore(name))
        raw = {w: sb(f"raw_{w}", [P, ots, kts * P]) for w, ots, kts in WEIGHTS}
        raw_fc1 = sb("raw_fc1", [HID, C])
        raw_fc2 = sb("raw_fc2", [P, CT, HID])
        raw_vec = sb("raw_vec", [NVEC * CT, P])
        vec = keep["vec"]
        taps = sb("taps", [P, CT, TAPS])
        root = sb("root", [P, 3 * CT])
        vare = sb("vare", [P, 3 * CT])
        inv = sb("inv", [P, 3 * CT])
        t0 = sb("t0", [P, 3 * CT])
        t1 = sb("t1", [P, 3 * CT])
        ps = [ctx.enter_context(nc.psum_tensor(f"ps{i}", [P, CH], F32)) for i in range(4)]

        loaded = sem("weights_loaded")
        ident_zero = sem("ident_zeroed")
        ident_ready = sem("ident_ready")
        turned = sem("weights_turned")
        copied = sem("turned_copied")
        var_ready = sem("variance_ready")
        root_ready = sem("root_ready")
        step = sem("dve_setup_step")
        done = sem("setup_done")
        block = ctx.enter_context(nc.Block())
        n_loads = len(WEIGHTS) + 2 + NVEC + 3

        @block.sync
        def _(sp):
            for w, ots, kts in WEIGHTS:
                sp.dma_start(raw[w][:, :, :], dram[w].rearrange("(t p) k -> p t k", p=P)).then_inc(loaded, 16)
            sp.dma_start(raw_fc1[:, :], dram["fc1"]).then_inc(loaded, 16)
            sp.dma_start(raw_fc2[:, :, :], dram["fc2"].rearrange("(t p) k -> p t k", p=P)).then_inc(loaded, 16)
            for i, v in enumerate(VEC):
                sp.dma_start(raw_vec[CT * i:CT * i + CT, :], dram[v].rearrange("(t p) -> t p", p=P)).then_inc(loaded, 16)
            sp.dma_start(taps[:, :, :], dram["edge_w"].rearrange("(t p) a h w -> p t (a h w)", p=P)).then_inc(loaded, 16)
            sp.dma_start(keep["dtaps"][:, :, :],
                         dram["deform_w"].rearrange("(t p) a h w -> p t (a h w)", p=P)).then_inc(loaded, 16)
            sp.dma_start(keep["bv"][:, :], dram["bv"].rearrange("(a k) -> a k", a=1).broadcast_to((P, C))).then_inc(loaded, 16)

        @block.gpsimd
        def _(pool):
            ident = keep["ident"]
            nc.gpsimd.memset(ident[:, :], 0.0).then_inc(ident_zero, 1)
            pool.wait_ge(ident_zero, 1)
            nc.gpsimd.affine_select(out=ident[:, :], in_=ident[:, :], compare_op=ALU.not_equal, fill=1.0,
                                    base=0, pattern=[[-1, P]], channel_multiplier=1).then_inc(ident_ready, 1)

        n_turned = 1 + len(blocks) + 2 * CT

        def turned_io(i):
            if i == 0:
                return raw_vec[:, :], vec[:, :, :].rearrange("p i t -> p (i t)"), NVEC * CT, P
            i -= 1
            if i < len(blocks):
                w, ot, kt = blocks[i]
                return raw[w][:, ot, kt * P:(kt + 1) * P], keep[w][:, kt, ot * P:(ot + 1) * P], P, P
            t = i - len(blocks)
            if t < CT:
                return raw_fc1[:, t * P:(t + 1) * P], keep["fc1"][:, t, :], HID, P
            return raw_fc2[:, t - CT, :], keep["fc2"][:, (t - CT) * P:(t - CT + 1) * P], P, HID

        @block.tensor
        def _(pe):
            pe.wait_ge(ident_ready, 1)
            pe.wait_ge(loaded, 16 * n_loads)
            for i in range(n_turned):
                src, _, rows, cols = turned_io(i)
                if i >= 4:
                    pe.wait_ge(copied, i - 3)
                nc.tensor.transpose(ps[i % 4][0:cols, 0:rows], src, keep["ident"][0:rows, 0:rows]).then_inc(turned, 1)

        @block.scalar
        def _(act):
            act.wait_ge(var_ready, 1)
            nc.scalar.activation(root[:, :], vare[:, :], ACT.Sqrt).then_inc(root_ready, 1)

        @block.vector
        def _(dve):
            n = [0]

            def link(ins):
                n[0] += 1
                ins.then_inc(step, 1)
                dve.wait_ge(step, n[0])

            def take(i):
                _, dst, rows, cols = turned_io(i)
                dve.wait_ge(turned, i + 1)
                nc.vector.tensor_copy(dst, ps[i % 4][0:cols, 0:rows]).then_inc(copied, 1)

            take(0)
            dve.wait_ge(copied, 1)
            col = lambda name: vec[:, VEC.index(name), :]
            link(nc.vector.tensor_scalar(keep["bqs"][:, 0, :], col("bq"), QS, None, ALU.mult))
            link(nc.vector.tensor_copy(keep["bqs"][:, 1, :], col("bk")))
            for j, (norm, _) in enumerate(NORMS):
                link(nc.vector.tensor_scalar(vare[:, CT * j:CT * j + CT], col(f"{norm}_var"), EPS, None, ALU.add))
            nc.vector.memset(t0[:, :], 1.5).then_inc(var_ready, 1)
            dve.wait_ge(root_ready, 1)
            link(nc.vector.reciprocal(inv[:, :], root[:, :]))
            link(nc.vector.tensor_tensor(t0[:, :], inv[:, :], inv[:, :], ALU.mult))
            link(nc.vector.tensor_tensor(t1[:, :], t0[:, :], vare[:, :], ALU.mult))
            link(nc.vector.tensor_scalar(t0[:, :], t1[:, :], -0.5, 1.5, ALU.mult, ALU.add))
            link(nc.vector.tensor_tensor(t1[:, :], t0[:, :], inv[:, :], ALU.mult))
            for j, (norm, bias) in enumerate(NORMS):
                s = keep["nscale"][:, j, :]
                o = keep["nshift"][:, j, :]
                tj = t0[:, CT * j:CT * j + CT]
                link(nc.vector.tensor_tensor(s, t1[:, CT * j:CT * j + CT], col(f"{norm}_gamma"), ALU.mult))
                link(nc.vector.tensor_tensor(tj, s, col(f"{norm}_mean"), ALU.mult))
                link(nc.vector.tensor_tensor(o, col(f"{norm}_beta"), tj, ALU.subtract))
                if bias:
                    link(nc.vector.tensor_tensor(tj, s, col(bias), ALU.mult))
                    link(nc.vector.tensor_tensor(o, o, tj, ALU.add))
            dve.wait_ge(ident_ready, 1)
            dve.wait_ge(loaded, 16 * n_loads)
            for t in range(CT):
                for k in range(TAPS):
                    nc.vector.tensor_scalar(keep["diag"][:, t, k, :], keep["ident"][:, :], taps[:, t, k:k + 1],
                                            None, ALU.mult)
            for i in range(1, n_turned):
                take(i)


def project_phase(nc, dram, keep, scratch):
    with ExitStack() as ctx:
        sb = lambda name, shape, dt=F32: ctx.enter_context(nc.sbuf_tensor(name, shape, dt))
        sem = lambda name: ctx.enter_context(nc.semaphore(name))
        x = [sb(f"x{p}", [P, CT, CH]) for p in range(2)]
        full = sb("full", [P, 4, CH])
        high = sb("high", [P, 4, CH], F32R)
        low = sb("low", [P, 4, CH], F32R)
        v1 = sb("v1", [P, HEADS, NSUB, 2, HD])
        pq = [ctx.enter_context(nc.psum_tensor(f"pq{k}", [P, CH], F32)) for k in range(4)]
        pv = [ctx.enter_context(nc.psum_tensor(f"pvp{k}", [P, 2, C], F32)) for k in range(2)]

        x_loaded = [sem(f"x_loaded{p}") for p in range(2)]
        x_used = sem("x_used")
        qk_ready = sem("qk_projected")
        v_ready = sem("v_projected")
        full_ready = sem("full_ready")
        high_ready = sem("high_ready")
        low_ready = sem("low_ready")
        ones_ready = sem("ones_ready")
        v_copied = sem("v_copied")
        qk_stored = sem("qk_stored")
        v_stored = sem("v_stored")
        block = ctx.enter_context(nc.Block())
        STEPS = B * NCH
        x_rows = dram["x"].rearrange("b (t p) h w -> p (b t) (h w)", p=P)

        @block.sync
        def _(sp):
            def load(b, c, p):
                sp.dma_start(x[p][:, :, :], x_rows[:, bass.ds(b * CT, CT), bass.ds(c * CH, CH)]).then_inc(x_loaded[p], 16)

            def store(b, c, n):
                sp.wait_ge(high_ready, 4 * n + 4)
                sp.wait_ge(low_ready, 4 * n + 4)
                for part, src in enumerate((high, low)):
                    for k in range(4):
                        for hpl in range(2):
                            row = ((b * 4 + (k % 2) * 2 + hpl) * 2 + part) * 2 + k // 2
                            sp.dma_start(scratch["qk"][bass.ds(row * 64, 64), bass.ds(c * CH, CH)],
                                         src[64 * hpl:64 * hpl + 64, k, :].bitcast(F32)).then_inc(qk_stored, 16)
                sp.wait_ge(v_copied, 2 * n + 2)
                sp.dma_start(scratch["v"][:, bass.ds(b * HEADS, HEADS), bass.ds(c * NSUB * 64, NSUB * 64)],
                             v1[:, :, :, :, :].rearrange("p h m a d -> p h (m a d)")).then_inc(v_stored, 16)

            load(0, 0, 0)
            load(0, 1, 1)
            with sp.Fori(0, B) as b:
                with sp.Fori(0, NCH // 2 - 1) as c2:
                    for p in range(2):
                        n = b * NCH + c2 * 2 + p
                        store(b, c2 * 2 + p, n)
                        sp.wait_ge(x_used, n + 1)
                        load(b, c2 * 2 + p + 2, p)
                for p in range(2):
                    c = NCH - 2 + p
                    n = b * NCH + c
                    store(b, c, n)
                    sp.wait_ge(x_used, n + 1)
                    load(B - 1, p, p)
            sp.wait_ge(qk_stored, 16 * 16 * STEPS)
            sp.wait_ge(v_stored, 16 * STEPS)
            for p in range(2):
                sp.wait_ge(x_loaded[p], 16 * (STEPS // 2 + 1))

        @block.tensor
        def _(pe):
            with pe.Fori(0, STEPS // 2) as i2:
                for p in range(2):
                    n = i2 * 2 + p
                    pe.wait_ge(x_loaded[p], 16 * i2 + 16)
                    pe.wait_ge(full_ready, 4 * n)
                    for k in range(4):
                        w = keep["wq" if k < 2 else "wk"]
                        ot = k % 2
                        for kt in range(CT):
                            mm = nc.tensor.matmul(pq[k][:, :], w[:, kt, ot * P:(ot + 1) * P], x[p][:, kt, :],
                                                  start=(kt == 0), stop=(kt == CT - 1))
                        mm.then_inc(qk_ready, 1)
                    pe.wait_ge(v_copied, 2 * n)
                    for j in range(2):
                        for s in range(2):
                            m = 2 * j + s
                            for kt in range(CT):
                                mm = nc.tensor.matmul(pv[j][:, s, :], x[p][:, kt, m * P:(m + 1) * P],
                                                      keep["wv"][:, kt, :],
                                                      start=(s == 0 and kt == 0), stop=(kt == CT - 1),
                                                      skip_group_check=True)
                        mm.then_inc(v_ready, 1)
                        if j == 1:
                            pe.drain().then_inc(x_used, 1)

        @block.scalar
        def _(act):
            with act.Fori(0, STEPS) as n:
                act.wait_ge(low_ready, 4 * n)
                for k in range(4):
                    act.wait_ge(qk_ready, 4 * n + k + 1)
                    nc.scalar.activation(full[:, k, :], pq[k][:, :], ACT.Identity, scale=QS if k < 2 else 1.0,
                                         bias=keep["bqs"][:, k // 2, k % 2:k % 2 + 1]).then_inc(full_ready, 1)

        @block.vector
        def _(dve):
            nc.vector.memset(v1[:, :, :, 1, :], 1.0).then_inc(ones_ready, 1)
            dve.wait_ge(ones_ready, 1)
            with dve.Fori(0, STEPS) as n:
                dve.wait_ge(qk_stored, 256 * n)
                for k in range(4):
                    dve.wait_ge(full_ready, 4 * n + k + 1)
                    nc.vector.tensor_copy(high[:, k, :], full[:, k, :]).then_inc(high_ready, 1)
                dve.wait_ge(v_stored, 16 * n)
                for j in range(2):
                    dve.wait_ge(v_ready, 2 * n + j + 1)
                    for s in range(2):
                        ins = nc.vector.tensor_tensor(
                            v1[:, :, 2 * j + s, 0, :], pv[j][:, s, :].rearrange("p (h d) -> p h d", h=HEADS),
                            keep["bv"][:, :].rearrange("p (h d) -> p h d", h=HEADS), ALU.add)
                    ins.then_inc(v_copied, 1)

        @block.gpsimd
        def _(pool):
            with pool.Fori(0, STEPS) as n:
                pool.wait_ge(qk_stored, 256 * n)
                for k in range(4):
                    pool.wait_ge(high_ready, 4 * n + k + 1)
                    nc.gpsimd.tensor_tensor(low[:, k, :], full[:, k, :], high[:, k, :].bitcast(F32),
                                            ALU.subtract).then_inc(low_ready, 1)


def attention_phase(nc, keep, scratch):
    with ExitStack() as ctx:
        sb = lambda name, shape, dt=F32: ctx.enter_context(nc.sbuf_tensor(name, shape, dt))
        sem = lambda name: ctx.enter_context(nc.semaphore(name))
        kk = [sb(f"keys{p}", [SPLIT + 1, 2, N], F32R) for p in range(2)]
        vv = [sb(f"values{p}", [P, 2, MT, 2 * HD]) for p in range(2)]
        qq = [sb(f"queries{p}", [SPLIT + 1, 2, CH], F32R) for p in range(2)]
        prob = [sb(f"prob{r}", [P, 2, CH]) for r in range(RING)]
        bmax = sb("block_max", [P, 2 * NSUB, MB])
        nmax = sb("negated_max", [P, 2 * NSUB])
        accs = sb("acc_copy", [P, CH])
        den = sb("den", [2 * HD, CH])
        num = sb("num", [2 * HD, CH])
        rec = sb("rec", [2 * HD, CH])
        fuse = [sb(f"fuse{p}", [2 * HD, CH]) for p in range(2)]
        st = [ctx.enter_context(nc.psum_tensor(f"st{i}", [P, 2, CH], F32)) for i in range(2)]
        mx = [ctx.enter_context(nc.psum_tensor(f"mx{i}", [P, CH], F32)) for i in range(2)]
        acc = ctx.enter_context(nc.psum_tensor("acc", [P, CH], F32))
        mrow = ctx.enter_context(nc.psum_tensor("mrow", [P, CH], F32))

        kv_loaded = [sem(f"kv_loaded{p}") for p in range(2)]
        q_loaded = [sem(f"q_loaded{p}") for p in range(2)]
        row_ones = sem("row_of_ones")
        scores = sem("scores_ready")
        exp_done = sem("exp_done")
        pv_done = sem("pv_done")
        mx_ready = sem("max_block_ready")
        mx_taken = sem("max_block_taken")
        nmax_ready = sem("negated_max_ready")
        mrow_ready = sem("max_row_ready")
        mrow_set = sem("max_row_set")
        acc_copied = sem("acc_copied")
        den_ready = sem("den_ready")
        rec_ready = sem("rec_ready")
        fuse_ready = sem("fuse_ready")
        fuse_stored = [sem(f"fuse_stored{p}") for p in range(2)]
        block = ctx.enter_context(nc.Block())

        KV_INC = 16 * 8
        Q_INC = 16 * 6

        @block.sync
        def _(sp):
            def load_kv(g, p):
                for h in range(2):
                    for r, part in enumerate((0, 1, 0)):
                        row = ((g * 2 + part) * 2 + 1) * 64 + h * HD
                        sp.dma_start(kk[p][r * HD:(r + 1) * HD, h, :].bitcast(F32),
                                     scratch["qk"][bass.ds(row, HD), :]).then_inc(kv_loaded[p], 16)
                    sp.dma_start(vv[p][:, h, :, :].rearrange("p m d -> p (m d)"),
                                 scratch["v"][:, bass.ds(g * 2 + h, 1), :].rearrange("p a k -> p (a k)")
                                 ).then_inc(kv_loaded[p], 16)

            def load_q(g, c, p):
                for h in range(2):
                    for r, part in enumerate((0, 0, 1)):
                        row = ((g * 2 + part) * 2) * 64 + h * HD
                        sp.dma_start(qq[p][r * HD:(r + 1) * HD, h, :].bitcast(F32),
                                     scratch["qk"][bass.ds(row, HD), bass.ds(c * CH, CH)]).then_inc(q_loaded[p], 16)

            def unit(g, c, gp, first, more_pairs):
                u = g * NCH + c
                if first and more_pairs:
                    sp.wait_ge(pv_done, MT * u)
                    load_kv(g + 1, 1 - gp)
                return u

            load_q(0, 0, 0)
            load_kv(0, 0)
            load_q(0, 1, 1)

            def pair(g, gp, more):
                sp.wait_ge(pv_done, MT * NCH * g)
                if more:
                    load_kv(g + 1, 1 - gp)
                with sp.Fori(0, NCH // 2 - 1) as c2:
                    for p in range(2):
                        u = g * NCH + c2 * 2 + p
                        sp.wait_ge(scores, MT * (u + 1))
                        load_q(g, c2 * 2 + p + 2, p)
                if more:
                    for p in range(2):
                        sp.wait_ge(scores, MT * (g * NCH + NCH - 2 + p + 1))
                        load_q(g + 1, p, p)

            with sp.Fori(0, PAIRS // 2 - 1) as g2:
                pair(g2 * 2, 0, True)
                pair(g2 * 2 + 1, 1, True)
            pair(PAIRS - 2, 0, True)
            pair(PAIRS - 1, 1, False)

        @block.tensor
        def _(pe):
            def score(p, gp, s):
                for h in range(2):
                    mm = nc.tensor.matmul(st[s % 2][:, h, :], kk[gp][:, h, s * P:(s + 1) * P], qq[p][:, h, :],
                                          start=True, stop=True)
                mm.then_inc(scores, 1)

            def max_block(p, gp, j, base):
                pe.wait_ge(mx_taken, base + (j - 1))
                hn, blk = j // MB, j % MB
                h, ns = hn // NSUB, hn % NSUB
                nc.tensor.matmul(mx[j % 2][:, :], qq[p][0:SPLIT, h, ns * P:(ns + 1) * P],
                                 kk[gp][0:SPLIT, h, blk * CH:(blk + 1) * CH],
                                 start=True, stop=True).then_inc(mx_ready, 1)

            def max_rows(v):
                pe.wait_ge(nmax_ready, v + 1)
                for h in range(2):
                    for ns in range(NSUB):
                        mm = nc.tensor.matmul(mrow[32 * h:32 * h + 1, ns * P:(ns + 1) * P],
                                              nmax[:, h * NSUB + ns:h * NSUB + ns + 1], keep["ident"][:, :],
                                              start=(ns == 0), stop=True, skip_group_check=True)
                mm.then_inc(mrow_ready, 1)

            def weigh(gp, s):
                for h in range(2):
                    mm = nc.tensor.matmul(acc[64 * h:64 * h + 64, :], vv[gp][:, h, s, :], prob[s % RING][:, h, :],
                                          start=(s == 0), stop=(s == MT - 1))
                mm.then_inc(pv_done, 1)

            first_step, last_step = 2, 27
            span = last_step - first_step + 1
            share = [[] for _ in range(MT)]
            for j in range(MAXMM):
                share[first_step + j * span // MAXMM].append(j)

            def unit(u, p, gp, ahead):
                pe.wait_ge(mrow_set, 2 * u + 2)
                for s in range(MT):
                    if s == 0:
                        pe.wait_ge(exp_done, MT * u)
                    elif s >= 2:
                        pe.wait_ge(exp_done, MT * u + s - 1)
                    score(p, gp, s)
                    if ahead:
                        ngp, waits = ahead
                        if s == first_step:
                            for w, value in waits:
                                pe.wait_ge(w, value)
                        for j in share[s]:
                            max_block(1 - p, ngp, j, MAXMM * (u + 1))
                        if s == MT - 3:
                            max_rows(u + 1)
                    if s >= 1:
                        if s == 1:
                            pe.wait_ge(acc_copied, u)
                        pe.wait_ge(exp_done, MT * u + s)
                        weigh(gp, s - 1)
                pe.wait_ge(exp_done, MT * u + MT)
                weigh(gp, MT - 1)

            def pair(g2, gp, more):
                g = g2 * 2 + gp
                nq = lambda c2: Q_INC * (g * (NCH // 2) + c2 + 1)
                with pe.Fori(0, NCH // 2 - 1) as c2:
                    unit(g * NCH + c2 * 2, 0, gp, (gp, [(q_loaded[1], nq(c2))]))
                    unit(g * NCH + c2 * 2 + 1, 1, gp, (gp, [(q_loaded[0], nq(c2 + 1))]))
                c2 = NCH // 2 - 1
                unit(g * NCH + c2 * 2, 0, gp, (gp, [(q_loaded[1], nq(c2))]))
                nk = KV_INC * (g2 + 1 + gp)
                unit(g * NCH + c2 * 2 + 1, 1, gp,
                     (1 - gp, [(q_loaded[0], nq(c2 + 1)), (kv_loaded[1 - gp], nk)]) if more else None)

            pe.wait_ge(row_ones, 2)
            pe.wait_ge(q_loaded[0], Q_INC)
            pe.wait_ge(kv_loaded[0], KV_INC)
            for j in range(MAXMM):
                if j < 2:
                    hn, blk = j // MB, j % MB
                    nc.tensor.matmul(mx[j][:, :], qq[0][0:SPLIT, 0, 0:P], kk[0][0:SPLIT, 0, blk * CH:(blk + 1) * CH],
                                     start=True, stop=True).then_inc(mx_ready, 1)
                else:
                    max_block(0, 0, j, 0)
            max_rows(0)
            with pe.Fori(0, PAIRS // 2 - 1) as g2:
                pair(g2, 0, True)
                pair(g2, 1, True)
            pair(PAIRS // 2 - 1, 0, True)
            pair(PAIRS // 2 - 1, 1, False)

        @block.scalar
        def _(act):
            with act.Fori(0, UNITS) as u:
                for s in range(MT):
                    act.wait_ge(scores, MT * u + s + 1)
                    if s == 0:
                        act.wait_ge(pv_done, MT * u)
                    elif s >= RING:
                        act.wait_ge(pv_done, MT * u + s - RING + 1)
                    nc.scalar.activation(prob[s % RING][:, :, :], st[s % 2][:, :, :], ACT.Exp).then_inc(exp_done, 1)

        @block.vector
        def _(dve):
            def maxima(v, p):
                for j in range(MAXMM):
                    dve.wait_ge(mx_ready, MAXMM * v + j + 1)
                    nc.vector.tensor_reduce(bmax[:, j // MB, j % MB:j % MB + 1], mx[j % 2][:, :], AX.X,
                                            ALU.max).then_inc(mx_taken, 1)
                dve.wait_ge(mx_taken, MAXMM * v + MAXMM)
                nc.vector.tensor_reduce(nmax[:, :], bmax[:, :, :], AX.X, ALU.max, negate=True).then_inc(nmax_ready, 1)
                dve.wait_ge(mrow_ready, v + 1)
                for h in range(2):
                    nc.vector.tensor_copy(qq[p][SPLIT:SPLIT + 1, h, :], mrow[32 * h:32 * h + 1, :]).then_inc(mrow_set, 1)

            def normalise(u, p, wait_store):
                dve.wait_ge(pv_done, MT * u + MT)
                nc.vector.tensor_copy(accs[:, :], acc[:, :]).then_inc(acc_copied, 1)
                dve.wait_ge(acc_copied, u + 1)
                for h in range(2):
                    nc.vector.tensor_copy(den[HD * h:HD * (h + 1), :], accs[64 * h + HD:64 * h + 64, :]).then_inc(den_ready, 1)
                    nc.vector.tensor_copy(num[HD * h:HD * (h + 1), :], accs[64 * h:64 * h + HD, :]).then_inc(den_ready, 1)
                dve.wait_ge(den_ready, 4 * u + 4)
                nc.vector.reciprocal(rec[:, :], den[:, :]).then_inc(rec_ready, 1)
                dve.wait_ge(rec_ready, u + 1)
                if wait_store is not None:
                    dve.wait_ge(fuse_stored[p], wait_store)
                nc.vector.tensor_tensor(fuse[p][:, :], num[:, :], rec[:, :], ALU.mult).then_inc(fuse_ready, 1)

            for p in range(2):
                nc.vector.memset(kk[p][SPLIT:SPLIT + 1, :, :].bitcast(F32), 1.0).then_inc(row_ones, 1)
            maxima(0, 0)
            with dve.Fori(0, UNITS // 2 - 1) as u2:
                maxima(u2 * 2 + 1, 1)
                normalise(u2 * 2, 0, 16 * u2)
                maxima(u2 * 2 + 2, 0)
                normalise(u2 * 2 + 1, 1, 16 * u2)
            maxima(UNITS - 1, 1)
            normalise(UNITS - 2, 0, 16 * (UNITS // 2 - 1))
            normalise(UNITS - 1, 1, 16 * (UNITS // 2 - 1))

        @block.gpsimd
        def _(pool):
            with pool.Fori(0, PAIRS) as g:
                with pool.Fori(0, NCH // 2) as c2:
                    for p in range(2):
                        pool.wait_ge(fuse_ready, g * NCH + c2 * 2 + p + 1)
                        pool.dma_start(scratch["fuse"][bass.ds(g * 64, 64), bass.ds((c2 * 2 + p) * CH, CH)],
                                       fuse[p][:, :]).then_inc(fuse_stored[p], 16)
            for p in range(2):
                pool.wait_ge(fuse_stored[p], 16 * UNITS // 2)


def image_phase(nc, dram, keep, scratch, out):
    with ExitStack() as ctx:
        sb = lambda name, shape, dt=F32: ctx.enter_context(nc.sbuf_tensor(name, shape, dt))
        sem = lambda name: ctx.enter_context(nc.semaphore(name))
        xf = [sb(f"xf{p}", [P, 2 * CT, CH]) for p in range(2)]
        m32 = sb("m32", [P, 32, 32])
        q32 = sb("q32", [P, 32, 32])
        m64 = sb("m64", [P, 32, WW])
        q64 = sb("q64", [P, 32, WW])
        mask = sb("mask", [P, HH, WW])
        diff = sb("diff", [P, CT, CH])
        y = sb("y", [P, CT, PR, PW])
        o1 = sb("o1", [P, CT, PR, PW])
        edge = [sb(f"edge{p}", [P, CT, CH]) for p in range(2)]
        dw = sb("dw", [P, CT, N])
        ysum = sb("ysum", [P, CT])
        hid = sb("hid", [HID, 1])
        nexp = sb("nexp", [P, CT])
        gate1 = sb("gate1", [P, CT])
        gate = sb("gate", [P, CT])
        fus = sb("fus", [P, CT, C])
        last = [sb(f"last{p}", [P, CT, CH]) for p in range(2)]
        bank = [ctx.enter_context(nc.psum_tensor(f"bank{i}", [P, CH], F32)) for i in range(8)]

        mask_loaded = sem("mask_loaded")
        mstep = sem("mask_step")
        xf_loaded = [sem(f"xf_loaded{p}") for p in range(2)]
        borders = sem("borders_zeroed")
        hybrid = sem("hybrid_ready")
        diffed = sem("diff_ready")
        masked = sem("masked_ready")
        y_ready = sem("y_ready")
        sum_ready = sem("sum_ready")
        hid_mm = sem("hidden_product")
        hid_ready = sem("hidden_ready")
        z_ready = sem("gate_product")
        nexp_ready = sem("gate_exp")
        gstep = sem("gate_step")
        edge_mm = sem("edge_product")
        edge_ready = sem("edge_ready")
        fus_mm = sem("fusion_product")
        o1_ready = sem("o1_ready")
        dwstep = sem("deform_step")
        bal_mm = sem("balance_product")
        last_ready = sem("last_ready")
        res_ready = sem("result_ready")
        stored = [sem(f"stored{p}") for p in range(2)]
        block = ctx.enter_context(nc.Block())

        x_rows = dram["x"].rearrange("b (t p) h w -> p (b t) (h w)", p=P)
        f_rows = scratch["fuse"].rearrange("(bt p) n -> p bt n", p=P)
        out_rows = out.rearrange("b (t p) h w -> p (b t) (h w)", p=P)

        def inner(t, ot, c, rows=ROWS, dy=1, dx=1):
            return t[:, ot, bass.ds(c * ROWS + dy, rows), dx:dx + WW]

        as_rows = lambda ap: ap.rearrange("p (r w) -> p r w", w=WW)

        @block.sync
        def _(sp):
            with sp.Fori(0, B) as b:
                sp.wait_ge(y_ready, 2 * NCH * b)
                sp.dma_start(m32[:, :, :].rearrange("p h w -> p (h w)"),
                             dram["mask"].rearrange("b a h w -> (b a) (h w)")[bass.ds(b, 1), :].broadcast_to((P, 1024))
                             ).then_inc(mask_loaded, 16)
                with sp.Fori(0, NCH // 2) as c2:
                    for p in range(2):
                        n = b * (NCH // 2) + c2
                        c = c2 * 2 + p
                        if p == 0:
                            sp.wait_ge(y_ready, 2 * NCH * b + 4 * c2)
                        sp.dma_start(xf[p][:, 0:CT, :], x_rows[:, bass.ds(b * CT, CT), bass.ds(c * CH, CH)]
                                     ).then_inc(xf_loaded[p], 16)
                        sp.dma_start(xf[p][:, CT:2 * CT, :], f_rows[:, bass.ds(b * CT, CT), bass.ds(c * CH, CH)]
                                     ).then_inc(xf_loaded[p], 16)
                with sp.Fori(0, NCH // 2) as c2:
                    for p in range(2):
                        c = c2 * 2 + p
                        sp.wait_ge(res_ready, 2 * (b * NCH + c) + 2)
                        sp.dma_start(out_rows[:, bass.ds(b * CT, CT), bass.ds(c * CH, CH)], last[p][:, :, :]
                                     ).then_inc(stored[p], 16)
            for p in range(2):
                sp.wait_ge(stored[p], 16 * B * NCH // 2)

        @block.tensor
        def _(pe):
            pe.wait_ge(borders, 2)
            with pe.Fori(0, B) as b:
                with pe.Fori(0, NCH // 2) as c2:
                    for p in range(2):
                        n = b * NCH + c2 * 2 + p
                        pe.wait_ge(xf_loaded[p], 32 * (b * (NCH // 2) + c2) + 32)
                        if p == 0:
                            pe.wait_ge(diffed, 2 * n)
                        for ot in range(CT):
                            for kt in range(2 * CT):
                                mm = nc.tensor.matmul(bank[2 * p + ot][:, :], keep["wf"][:, kt, ot * P:(ot + 1) * P],
                                                      xf[p][:, kt, :], start=(kt == 0), stop=(kt == 2 * CT - 1))
                            mm.then_inc(hybrid, 1)
                pe.wait_ge(sum_ready, 2 * b + 2)
                for kt in range(CT):
                    mm = nc.tensor.matmul(bank[4][0:HID, 0:1], keep["fc1"][:, kt, :], ysum[:, kt:kt + 1],
                                          start=(kt == 0), stop=(kt == CT - 1))
                mm.then_inc(hid_mm, 1)
                pe.wait_ge(hid_ready, b + 1)
                for ot in range(CT):
                    mm = nc.tensor.matmul(bank[5][:, ot:ot + 1], keep["fc2"][:, ot * P:(ot + 1) * P], hid[:, :],
                                          start=(ot == 0), stop=True, skip_group_check=True)
                mm.then_inc(z_ready, 1)
                with pe.Fori(0, NCH // 2) as c2:
                    for p in range(2):
                        n = b * NCH + c2 * 2 + p
                        c = c2 * 2 + p
                        pe.wait_ge(gstep, 4 * b + 4)
                        pe.wait_ge(edge_ready, 2 * n)
                        for ct in range(CT):
                            for k in range(TAPS):
                                mm = nc.tensor.matmul(as_rows(bank[ct][:, :]), keep["diag"][:, ct, k, :],
                                                      inner(y, ct, c, dy=k // 3, dx=k % 3),
                                                      start=(k == 0), stop=(k == TAPS - 1))
                            mm.then_inc(edge_mm, 1)
                        pe.wait_ge(o1_ready, 2 * n)
                        pe.wait_ge(edge_ready, 2 * n + 2)
                        for ot in range(CT):
                            for kt in range(CT):
                                nc.tensor.matmul(as_rows(bank[2 + ot][:, :]), fus[:, kt, ot * P:(ot + 1) * P],
                                                 inner(y, kt, c), start=(kt == 0), stop=False)
                            for kt in range(CT):
                                mm = nc.tensor.matmul(as_rows(bank[2 + ot][:, :]),
                                                      keep["fu"][:, CT + kt, ot * P:(ot + 1) * P],
                                                      as_rows(edge[p][:, kt, :]), start=False, stop=(kt == CT - 1))
                            mm.then_inc(fus_mm, 1)
                with pe.Fori(0, NCH // 2) as c2:
                    for p in range(2):
                        n = b * NCH + c2 * 2 + p
                        c = c2 * 2 + p
                        if p == 0:
                            pe.wait_ge(last_ready, 2 * n)
                        pe.wait_ge(dwstep, CT * TAPS * (n + 1))
                        for ot in range(CT):
                            for kt in range(CT):
                                mm = nc.tensor.matmul(bank[4 + 2 * p + ot][:, :], keep["ba"][:, kt, ot * P:(ot + 1) * P],
                                                      dw[:, kt, bass.ds(c * CH, CH)],
                                                      start=(kt == 0), stop=(kt == CT - 1))
                            mm.then_inc(bal_mm, 1)

        @block.scalar
        def _(act):
            with act.Fori(0, B) as b:
                act.wait_ge(hid_mm, b + 1)
                nc.scalar.activation(hid[:, :], bank[4][0:HID, 0:1], ACT.Relu, scale=1.0 / N).then_inc(hid_ready, 1)
                act.wait_ge(z_ready, b + 1)
                nc.scalar.activation(nexp[:, :], bank[5][:, 0:CT], ACT.Exp, scale=-1.0).then_inc(nexp_ready, 1)
                with act.Fori(0, NCH // 2) as c2:
                    for p in range(2):
                        n = b * NCH + c2 * 2 + p
                        c = c2 * 2 + p
                        for ct in range(CT):
                            act.wait_ge(edge_mm, 2 * n + ct + 1)
                            nc.scalar.activation(edge[p][:, ct, :], bank[ct][:, :], ACT.Relu,
                                                 scale=keep["nscale"][:, 0, ct:ct + 1],
                                                 bias=keep["nshift"][:, 0, ct:ct + 1]).then_inc(edge_ready, 1)
                        for ot in range(CT):
                            act.wait_ge(fus_mm, 2 * n + ot + 1)
                            nc.scalar.activation(inner(o1, ot, c), as_rows(bank[2 + ot][:, :]), ACT.Identity,
                                                 scale=keep["nscale"][:, 1, ot:ot + 1],
                                                 bias=keep["nshift"][:, 1, ot:ot + 1]).then_inc(o1_ready, 1)
                with act.Fori(0, NCH // 2) as c2:
                    for p in range(2):
                        n = b * NCH + c2 * 2 + p
                        act.wait_ge(stored[p], 16 * (b * (NCH // 2) + c2))
                        for ot in range(CT):
                            act.wait_ge(bal_mm, 2 * n + ot + 1)
                            nc.scalar.activation(last[p][:, ot, :], bank[4 + 2 * p + ot][:, :], ACT.Identity,
                                                 scale=keep["nscale"][:, 2, ot:ot + 1],
                                                 bias=keep["nshift"][:, 2, ot:ot + 1]).then_inc(last_ready, 1)

        @block.gpsimd
        def _(pool):
            nc.gpsimd.memset(y[:, :, :, :].rearrange("p t r w -> p (t r w)"), 0.0).then_inc(borders, 1)
            nc.gpsimd.memset(o1[:, :, :, :].rearrange("p t r w -> p (t r w)"), 0.0).then_inc(borders, 1)

        @block.vector
        def _(dve):
            NM = 10

            def upsample(b):
                n = [0]

                def link(ins):
                    n[0] += 1
                    ins.then_inc(mstep, 1)
                    if n[0] < NM:
                        dve.wait_ge(mstep, b * NM + n[0])

                link(nc.vector.tensor_scalar(q32[:, :, :], m32[:, :, :], 0.25, None, ALU.mult))
                cols = m64[:, :, :].rearrange("p h (w a) -> p h w a", a=2)
                link(nc.vector.scalar_tensor_tensor(out=cols[:, :, 1:32, 0], in0=m32[:, :, 1:32], scalar=0.75,
                                                    in1=q32[:, :, 0:31], op0=ALU.mult, op1=ALU.add))
                link(nc.vector.scalar_tensor_tensor(out=cols[:, :, 0:31, 1], in0=m32[:, :, 0:31], scalar=0.75,
                                                    in1=q32[:, :, 1:32], op0=ALU.mult, op1=ALU.add))
                link(nc.vector.tensor_copy(cols[:, :, 0, 0], m32[:, :, 0]))
                link(nc.vector.tensor_copy(cols[:, :, 31, 1], m32[:, :, 31]))
                link(nc.vector.tensor_scalar(q64[:, :, :], m64[:, :, :], 0.25, None, ALU.mult))
                rows = mask[:, :, :].rearrange("p (h a) w -> p h a w", a=2)
                link(nc.vector.scalar_tensor_tensor(out=rows[:, 1:32, 0, :], in0=m64[:, 1:32, :], scalar=0.75,
                                                    in1=q64[:, 0:31, :], op0=ALU.mult, op1=ALU.add))
                link(nc.vector.scalar_tensor_tensor(out=rows[:, 0:31, 1, :], in0=m64[:, 0:31, :], scalar=0.75,
                                                    in1=q64[:, 1:32, :], op0=ALU.mult, op1=ALU.add))
                link(nc.vector.tensor_copy(rows[:, 0, 0, :], m64[:, 0, :]))
                link(nc.vector.tensor_copy(rows[:, 31, 1, :], m64[:, 31, :]))

            dve.wait_ge(borders, 2)
            with dve.Fori(0, B) as b:
                dve.wait_ge(mask_loaded, 16 * b + 16)
                upsample(b)
                with dve.Fori(0, NCH // 2) as c2:
                    for p in range(2):
                        n = b * NCH + c2 * 2 + p
                        c = c2 * 2 + p
                        for ot in range(CT):
                            dve.wait_ge(hybrid, 2 * n + ot + 1)
                            dve.wait_ge(y_ready, 2 * n)
                            nc.vector.scalar_tensor_tensor(
                                out=diff[:, ot, :], in0=bank[2 * p + ot][:, :],
                                scalar=keep["vec"][:, VEC.index("bf"), ot:ot + 1], in1=xf[p][:, ot, :],
                                op0=ALU.add, op1=ALU.subtract).then_inc(diffed, 1)
                        for ot in range(CT):
                            dve.wait_ge(diffed, 2 * n + ot + 1)
                            dve.wait_ge(mstep, NM * b + NM)
                            nc.vector.tensor_tensor(as_rows(diff[:, ot, :]), as_rows(diff[:, ot, :]),
                                                    mask[:, bass.ds(c * ROWS, ROWS), :], ALU.mult).then_inc(masked, 1)
                        for ot in range(CT):
                            dve.wait_ge(masked, 2 * n + ot + 1)
                            nc.vector.tensor_tensor(inner(y, ot, c), as_rows(diff[:, ot, :]),
                                                    as_rows(xf[p][:, ot, :]), ALU.add).then_inc(y_ready, 1)
                dve.wait_ge(y_ready, 2 * NCH * (b + 1))
                for ct in range(CT):
                    nc.vector.tensor_reduce(ysum[:, ct:ct + 1], y[:, ct, 1:1 + HH, 1:1 + WW], AX.XY,
                                            ALU.add).then_inc(sum_ready, 1)
                dve.wait_ge(nexp_ready, b + 1)
                nc.vector.tensor_scalar(gate1[:, :], nexp[:, :], 1.0, None, ALU.add).then_inc(gstep, 1)
                dve.wait_ge(gstep, 4 * b + 1)
                nc.vector.reciprocal(gate[:, :], gate1[:, :]).then_inc(gstep, 1)
                dve.wait_ge(gstep, 4 * b + 2)
                for kt in range(CT):
                    nc.vector.tensor_scalar(fus[:, kt, :], keep["fu"][:, kt, :], gate[:, kt:kt + 1], None,
                                            ALU.mult).then_inc(gstep, 1)

                def deform(c, last_c):
                    n = b * NCH + c
                    dve.wait_ge(o1_ready, 2 * n + (2 if last_c else 4))
                    for k in range(TAPS):
                        for ct in range(CT):
                            dst = as_rows(dw[:, ct, bass.ds(c * CH, CH)])
                            src = inner(o1, ct, c, dy=k // 3, dx=k % 3)
                            w = keep["dtaps"][:, ct, k:k + 1]
                            at = CT * TAPS * n + CT * k + ct
                            if k == 0:
                                ins = nc.vector.tensor_scalar(dst, src, w, None, ALU.mult)
                            else:
                                dve.wait_ge(dwstep, at - 1)
                                ins = nc.vector.scalar_tensor_tensor(out=dst, in0=src, scalar=w, in1=dst,
                                                                     op0=ALU.mult, op1=ALU.add)
                            ins.then_inc(dwstep, 1)

                with dve.Fori(0, NCH - 1) as c:
                    deform(c, False)
                deform(NCH - 1, True)
                with dve.Fori(0, NCH // 2) as c2:
                    for p in range(2):
                        c = c2 * 2 + p
                        for ot in range(CT):
                            dve.wait_ge(last_ready, 2 * (b * NCH + c) + ot + 1)
                            nc.vector.tensor_tensor(as_rows(last[p][:, ot, :]), as_rows(last[p][:, ot, :]),
                                                    inner(y, ot, c), ALU.mult).then_inc(res_ready, 1)


def build(nc, dram, out):
    with ExitStack() as ctx:
        sb = lambda name, shape: ctx.enter_context(nc.sbuf_tensor(name, shape, F32))
        keep = {
            "ident": sb("ident", [P, P]),
            "vec": sb("vec", [P, NVEC, CT]),
            "bqs": sb("bqs", [P, 2, CT]),
            "bv": sb("bv_rows", [P, C]),
            "nscale": sb("nscale", [P, 3, CT]),
            "nshift": sb("nshift", [P, 3, CT]),
            "dtaps": sb("dtaps", [P, CT, TAPS]),
            "diag": sb("diag", [P, CT, TAPS, P]),
            "fc1": sb("fc1T", [P, CT, HID]),
            "fc2": sb("fc2T", [HID, C]),
        }
        for w, ots, kts in WEIGHTS:
            keep[w] = sb(f"{w}T", [P, kts, ots * P])
        scratch = {
            "qk": nc.dram_tensor("qk_scratch", [PAIRS * 2 * 2 * 64, N], F32).ap(),
            "v": nc.dram_tensor("v_scratch", [P, B * HEADS, MT * 64], F32).ap(),
            "fuse": nc.dram_tensor("fuse_scratch", [B * C, N], F32).ap(),
        }
        setup_phase(nc, dram, keep)
        project_phase(nc, dram, keep, scratch)
        attention_phase(nc, keep, scratch)
        image_phase(nc, dram, keep, scratch, out)


_INS = {
    "x": "x", "mask": "L0_conv_mask", "wq": "L0_conv_Wq", "bq": "L0_conv_bq", "wk": "L0_conv_Wk", "bk": "L0_conv_bk",
    "wv": "L0_conv_Wv", "bv": "L0_conv_bv", "wf": "L0_conv_Wf", "bf": "L0_conv_bf",
    "edge_w": "L1_conv_edge_w", "edge_gamma": "L1_conv_edge_gamma", "edge_beta": "L1_conv_edge_beta",
    "edge_mean": "L1_conv_edge_mean", "edge_var": "L1_conv_edge_var", "fc1": "L1_conv_fc1_w", "fc2": "L1_conv_fc2_w",
    "fu": "L1_conv_fusion_w", "fusion_b": "L1_conv_fusion_b", "bn1_gamma": "L1_conv_bn1_gamma",
    "bn1_beta": "L1_conv_bn1_beta", "bn1_mean": "L1_conv_bn1_mean", "bn1_var": "L1_conv_bn1_var",
    "deform_w": "L1_conv_deform_w", "ba": "L1_conv_balance_w", "balance_b": "L1_conv_balance_b",
    "bn2_gamma": "L1_conv_bn2_gamma", "bn2_beta": "L1_conv_bn2_beta", "bn2_mean": "L1_conv_bn2_mean",
    "bn2_var": "L1_conv_bn2_var",
}


def kernel(**inputs):
    import numpy as _np
    import concourse.bacc as _bacc
    from concourse import mybir as _mybir
    from concourse.bass_utils import run_bass_kernel_spmd as _run

    nc = _bacc.Bacc("TRN2", target_bir_lowering=False, num_devices=1)
    arrays, dram = {}, {}
    for short, name in _INS.items():
        a = _np.ascontiguousarray(inputs[name])
        arrays[f"in_{name}"] = a
        dram[short] = nc.dram_tensor(f"in_{name}", a.shape, _mybir.dt.from_np(a.dtype), kind="ExternalInput").ap()
    out = nc.dram_tensor("out_dram", (B, C, HH, WW), F32, kind="ExternalOutput").ap()
    build(nc, dram, out)
    r = _run(nc, [arrays], core_ids=[0])
    return r.results[0]["out_dram"]
```

```python
from contextlib import ExitStack

import concourse.bass as bass
from concourse import mybir

F32 = mybir.dt.float32
F32R = mybir.dt.float32r
ALU = mybir.AluOpType
ACT = mybir.ActivationFunctionType
AX = mybir.AxisListType

P = 128
B, C, HH, WW = 2, 256, 64, 64
N = HH * WW
CT = C // P
HEADS = 8
HD = C // HEADS
QS = float(HD) ** -0.5
CH = 512
NCH = N // CH
MT = N // P
PAIRS = B * HEADS // 2
UNITS = PAIRS * NCH
ROWS = CH // WW
PW = WW + 2
PR = HH + 2
SPLIT = 3 * HD
NSUB = CH // P
MB = N // CH
MAXMM = 2 * NSUB * MB
EPS = 1e-5
HID = C // 16
TAPS = 9

VEC = ["bq", "bk", "bf", "edge_gamma", "edge_beta", "edge_mean", "edge_var", "fusion_b",
       "bn1_gamma", "bn1_beta", "bn1_mean", "bn1_var", "balance_b",
       "bn2_gamma", "bn2_beta", "bn2_mean", "bn2_var"]
NVEC = len(VEC)
NORMS = [("edge", None), ("bn1", "fusion_b"), ("bn2", "balance_b")]
WEIGHTS = [("wq", CT, CT), ("wk", CT, CT), ("wv", CT, CT), ("wf", CT, 2 * CT), ("fu", CT, 2 * CT), ("ba", CT, CT)]


def setup_phase(nc, dram, keep):
    blocks = [(w, ot, kt) for w, ots, kts in WEIGHTS for ot in range(ots) for kt in range(kts)]
    with ExitStack() as ctx:
        sb = lambda name, shape, dt=F32: ctx.enter_context(nc.sbuf_tensor(name, shape, dt))
        sem = lambda name: ctx.enter_context(nc.semaphore(name))
        raw = {w: sb(f"raw_{w}", [P, ots, kts * P]) for w, ots, kts in WEIGHTS}
        raw_fc1 = sb("raw_fc1", [HID, C])
        raw_fc2 = sb("raw_fc2", [P, CT, HID])
        raw_vec = sb("raw_vec", [NVEC * CT, P])
        vec = keep["vec"]
        taps = sb("taps", [P, CT, TAPS])
        root = sb("root", [P, 3 * CT])
        vare = sb("vare", [P, 3 * CT])
        inv = sb("inv", [P, 3 * CT])
        t0 = sb("t0", [P, 3 * CT])
        t1 = sb("t1", [P, 3 * CT])
        ps = [ctx.enter_context(nc.psum_tensor(f"ps{i}", [P, CH], F32)) for i in range(4)]

        loaded = sem("weights_loaded")
        ident_zero = sem("ident_zeroed")
        ident_ready = sem("ident_ready")
        turned = sem("weights_turned")
        copied = sem("turned_copied")
        var_ready = sem("variance_ready")
        root_ready = sem("root_ready")
        step = sem("dve_setup_step")
        done = sem("setup_done")
        block = ctx.enter_context(nc.Block())
        n_loads = len(WEIGHTS) + 2 + NVEC + 3

        @block.sync
        def _(sp):
            for w, ots, kts in WEIGHTS:
                sp.dma_start(raw[w][:, :, :], dram[w].rearrange("(t p) k -> p t k", p=P)).then_inc(loaded, 16)
            sp.dma_start(raw_fc1[:, :], dram["fc1"]).then_inc(loaded, 16)
            sp.dma_start(raw_fc2[:, :, :], dram["fc2"].rearrange("(t p) k -> p t k", p=P)).then_inc(loaded, 16)
            for i, v in enumerate(VEC):
                sp.dma_start(raw_vec[CT * i:CT * i + CT, :], dram[v].rearrange("(t p) -> t p", p=P)).then_inc(loaded, 16)
            sp.dma_start(taps[:, :, :], dram["edge_w"].rearrange("(t p) a h w -> p t (a h w)", p=P)).then_inc(loaded, 16)
            sp.dma_start(keep["dtaps"][:, :, :],
                         dram["deform_w"].rearrange("(t p) a h w -> p t (a h w)", p=P)).then_inc(loaded, 16)
            sp.dma_start(keep["bv"][:, :], dram["bv"].rearrange("(a k) -> a k", a=1).broadcast_to((P, C))).then_inc(loaded, 16)

        @block.gpsimd
        def _(pool):
            ident = keep["ident"]
            nc.gpsimd.memset(ident[:, :], 0.0).then_inc(ident_zero, 1)
            pool.wait_ge(ident_zero, 1)
            nc.gpsimd.affine_select(out=ident[:, :], in_=ident[:, :], compare_op=ALU.not_equal, fill=1.0,
                                    base=0, pattern=[[-1, P]], channel_multiplier=1).then_inc(ident_ready, 1)

        n_turned = 1 + len(blocks) + 2 * CT

        def turned_io(i):
            if i == 0:
                return raw_vec[:, :], vec[:, :, :].rearrange("p i t -> p (i t)"), NVEC * CT, P
            i -= 1
            if i < len(blocks):
                w, ot, kt = blocks[i]
                return raw[w][:, ot, kt * P:(kt + 1) * P], keep[w][:, kt, ot * P:(ot + 1) * P], P, P
            t = i - len(blocks)
            if t < CT:
                return raw_fc1[:, t * P:(t + 1) * P], keep["fc1"][:, t, :], HID, P
            return raw_fc2[:, t - CT, :], keep["fc2"][:, (t - CT) * P:(t - CT + 1) * P], P, HID

        @block.tensor
        def _(pe):
            pe.wait_ge(ident_ready, 1)
            pe.wait_ge(loaded, 16 * n_loads)
            for i in range(n_turned):
                src, _, rows, cols = turned_io(i)
                if i >= 4:
                    pe.wait_ge(copied, i - 3)
                nc.tensor.transpose(ps[i % 4][0:cols, 0:rows], src, keep["ident"][0:rows, 0:rows]).then_inc(turned, 1)

        @block.scalar
        def _(act):
            act.wait_ge(var_ready, 1)
            nc.scalar.activation(root[:, :], vare[:, :], ACT.Sqrt).then_inc(root_ready, 1)

        @block.vector
        def _(dve):
            n = [0]

            def link(ins):
                n[0] += 1
                ins.then_inc(step, 1)
                dve.wait_ge(step, n[0])

            def take(i):
                _, dst, rows, cols = turned_io(i)
                dve.wait_ge(turned, i + 1)
                nc.vector.tensor_copy(dst, ps[i % 4][0:cols, 0:rows]).then_inc(copied, 1)

            take(0)
            dve.wait_ge(copied, 1)
            col = lambda name: vec[:, VEC.index(name), :]
            link(nc.vector.tensor_scalar(keep["bqs"][:, 0, :], col("bq"), QS, None, ALU.mult))
            link(nc.vector.tensor_copy(keep["bqs"][:, 1, :], col("bk")))
            for j, (norm, _) in enumerate(NORMS):
                link(nc.vector.tensor_scalar(vare[:, CT * j:CT * j + CT], col(f"{norm}_var"), EPS, None, ALU.add))
            nc.vector.memset(t0[:, :], 1.5).then_inc(var_ready, 1)
            dve.wait_ge(root_ready, 1)
            link(nc.vector.reciprocal(inv[:, :], root[:, :]))
            link(nc.vector.tensor_tensor(t0[:, :], inv[:, :], inv[:, :], ALU.mult))
            link(nc.vector.tensor_tensor(t1[:, :], t0[:, :], vare[:, :], ALU.mult))
            link(nc.vector.tensor_scalar(t0[:, :], t1[:, :], -0.5, 1.5, ALU.mult, ALU.add))
            link(nc.vector.tensor_tensor(t1[:, :], t0[:, :], inv[:, :], ALU.mult))
            for j, (norm, bias) in enumerate(NORMS):
                s = keep["nscale"][:, j, :]
                o = keep["nshift"][:, j, :]
                tj = t0[:, CT * j:CT * j + CT]
                link(nc.vector.tensor_tensor(s, t1[:, CT * j:CT * j + CT], col(f"{norm}_gamma"), ALU.mult))
                link(nc.vector.tensor_tensor(tj, s, col(f"{norm}_mean"), ALU.mult))
                link(nc.vector.tensor_tensor(o, col(f"{norm}_beta"), tj, ALU.subtract))
                if bias:
                    link(nc.vector.tensor_tensor(tj, s, col(bias), ALU.mult))
                    link(nc.vector.tensor_tensor(o, o, tj, ALU.add))
            dve.wait_ge(ident_ready, 1)
            dve.wait_ge(loaded, 16 * n_loads)
            for t in range(CT):
                for k in range(TAPS):
                    nc.vector.tensor_scalar(keep["diag"][:, t, k, :], keep["ident"][:, :], taps[:, t, k:k + 1],
                                            None, ALU.mult)
            for i in range(1, n_turned):
                take(i)


def project_phase(nc, dram, keep, scratch):
    with ExitStack() as ctx:
        sb = lambda name, shape, dt=F32: ctx.enter_context(nc.sbuf_tensor(name, shape, dt))
        sem = lambda name: ctx.enter_context(nc.semaphore(name))
        x = [sb(f"x{p}", [P, CT, CH]) for p in range(2)]
        full = sb("full", [P, 4, CH])
        high = sb("high", [P, 4, CH], F32R)
        low = sb("low", [P, 4, CH], F32R)
        v1 = sb("v1", [P, HEADS, NSUB, HD])
        pq = [ctx.enter_context(nc.psum_tensor(f"pq{k}", [P, CH], F32)) for k in range(4)]
        pv = [ctx.enter_context(nc.psum_tensor(f"pvp{k}", [P, 2, C], F32)) for k in range(2)]

        x_loaded = [sem(f"x_loaded{p}") for p in range(2)]
        x_used = sem("x_used")
        qk_ready = sem("qk_projected")
        v_ready = sem("v_projected")
        full_ready = sem("full_ready")
        high_ready = sem("high_ready")
        low_ready = sem("low_ready")
        v_copied = sem("v_copied")
        qk_stored = sem("qk_stored")
        v_stored = sem("v_stored")
        block = ctx.enter_context(nc.Block())
        STEPS = B * NCH
        STORES = 16
        x_rows = dram["x"].rearrange("b (t p) h w -> p (b t) (h w)", p=P)


        @block.sync
        def _(sp):
            sp.sem_inc(qk_stored, 16 * STORES)
            sp.sem_inc(v_stored, 16)

            def load(b, c, p):
                sp.dma_start(x[p][:, :, :], x_rows[:, bass.ds(b * CT, CT), bass.ds(c * CH, CH)]).then_inc(x_loaded[p], 16)

            def store(b, c, n):
                sp.wait_ge(high_ready, 4 * n + 4)
                sp.wait_ge(low_ready, 4 * (n + 1) + 4)
                for part, src in enumerate((high, low)):
                    for t in range(CT):
                        for hpl in range(2):
                            g = b * (HEADS // 2) + t * 2 + hpl
                            sp.dma_start(scratch["q"][bass.ds(g * NCH + c, 1), part, :, :].rearrange("a r n -> (a r) n"),
                                         src[64 * hpl:64 * hpl + 64, t, :].bitcast(F32)).then_inc(qk_stored, 16)
                            sp.dma_start(scratch["k"][bass.ds((g * 2 + part) * 64, 64), bass.ds(c * CH, CH)],
                                         src[64 * hpl:64 * hpl + 64, CT + t, :].bitcast(F32)).then_inc(qk_stored, 16)
                sp.wait_ge(v_copied, 2 * (n + 1) + 2)
                sp.dma_start(scratch["v"][:, bass.ds(b * HEADS, HEADS), bass.ds(c * NSUB * HD, NSUB * HD)],
                             v1[:, :, :, :].rearrange("p h m d -> p h (m d)")).then_inc(v_stored, 16)

            load(0, 0, 0)
            load(0, 1, 1)
            with sp.Fori(0, B) as b:
                with sp.Fori(0, NCH // 2 - 1) as c2:
                    for p in range(2):
                        n = b * NCH + c2 * 2 + p
                        store(b, c2 * 2 + p, n)
                        sp.wait_ge(x_used, n + 1)
                        load(b, c2 * 2 + p + 2, p)
                for p in range(2):
                    c = NCH - 2 + p
                    n = b * NCH + c
                    store(b, c, n)
                    sp.wait_ge(x_used, n + 1)
                    load(B - 1, p, p)
            sp.wait_ge(qk_stored, 16 * STORES * (STEPS + 1))
            sp.wait_ge(v_stored, 16 * (STEPS + 1))
            for p in range(2):
                sp.wait_ge(x_loaded[p], 16 * (STEPS // 2 + 1))

        @block.tensor
        def _(pe):
            with pe.Fori(0, STEPS // 2) as i2:
                for p in range(2):
                    n = i2 * 2 + p
                    pe.wait_ge(x_loaded[p], 16 * i2 + 16)
                    pe.wait_ge(full_ready, 4 * (n + 1))
                    for k in range(4):
                        w = keep["wq" if k < 2 else "wk"]
                        ot = k % 2
                        for kt in range(CT):
                            mm = nc.tensor.matmul(pq[k][:, :], w[:, kt, ot * P:(ot + 1) * P], x[p][:, kt, :],
                                                  start=(kt == 0), stop=(kt == CT - 1))
                        mm.then_inc(qk_ready, 1)
                    pe.wait_ge(v_copied, 2 * (n + 1))
                    for j in range(2):
                        for s in range(2):
                            m = 2 * j + s
                            for kt in range(CT):
                                mm = nc.tensor.matmul(pv[j][:, s, :], x[p][:, kt, m * P:(m + 1) * P],
                                                      keep["wv"][:, kt, :],
                                                      start=(s == 0 and kt == 0), stop=(kt == CT - 1),
                                                      skip_group_check=True)
                        mm.then_inc(v_ready, 1)
                        if j == 1:
                            pe.drain().then_inc(x_used, 1)

        @block.scalar
        def _(act):
            act.sem_inc(full_ready, 4)
            with act.Fori(0, STEPS) as n:
                act.wait_ge(low_ready, 4 * (n + 1))
                for k in range(4):
                    act.wait_ge(qk_ready, 4 * n + k + 1)
                    nc.scalar.activation(full[:, k, :], pq[k][:, :], ACT.Identity, scale=QS if k < 2 else 1.0,
                                         bias=keep["bqs"][:, k // 2, k % 2:k % 2 + 1]).then_inc(full_ready, 1)

        @block.vector
        def _(dve):
            dve.sem_inc(v_copied, 2)
            with dve.Fori(0, STEPS) as n:
                dve.wait_ge(qk_stored, 16 * STORES * (n + 1))
                for k in range(4):
                    dve.wait_ge(full_ready, 4 * (n + 1) + k + 1)
                    nc.vector.tensor_copy(high[:, k, :], full[:, k, :]).then_inc(high_ready, 1)
                dve.wait_ge(v_stored, 16 * (n + 1))
                for j in range(2):
                    dve.wait_ge(v_ready, 2 * n + j + 1)
                    for s in range(2):
                        ins = nc.vector.tensor_tensor(
                            v1[:, :, 2 * j + s, :], pv[j][:, s, :].rearrange("p (h d) -> p h d", h=HEADS),
                            keep["bv"][:, :].rearrange("p (h d) -> p h d", h=HEADS), ALU.add)
                    ins.then_inc(v_copied, 1)

        @block.gpsimd
        def _(pool):
            pool.sem_inc(low_ready, 4)
            with pool.Fori(0, STEPS) as n:
                pool.wait_ge(qk_stored, 16 * STORES * (n + 1))
                for k in range(4):
                    pool.wait_ge(high_ready, 4 * n + k + 1)
                    nc.gpsimd.tensor_tensor(low[:, k, :], full[:, k, :], high[:, k, :].bitcast(F32),
                                            ALU.subtract).then_inc(low_ready, 1)


GROUPS = [3, 3, 2, 3, 3, 3, 3, 2, 3, 3]
GROUP_END = [sum(GROUPS[:k + 1]) for k in range(len(GROUPS))]
PLAIN = MT - sum(GROUPS)
ADDS = sum(GROUPS) - len(GROUPS)
QUADS = MT // 2
SUMS = (len(GROUPS) + PLAIN) // 2
SUM_STEP = [9, 14, 20, 25]
SUM_ORDER = [0, 1, 2, 3, 5, 4, 6]
SUM_COUNT = [SUM_ORDER.index(i) + 1 for i in range(SUMS)]
SUM_BUFS = 5
BANKS = 3
TILES = 2 * MT
RING = 8
V_LAG = 3
T_ONE, T_QUAD, T_REDUCE, T_SEEN, T_HANDOVER = 0.215, 1.0, 0.6, 0.2, 0.27
TAKE_NUM, TAKE_DEN, INVERT = 2, 6, 24
T_BETWEEN = {TAKE_NUM: 0.65, TAKE_DEN: 0.65, INVERT: 0.15}


def attention_phase(nc, keep, scratch):
    with ExitStack() as ctx:
        sb = lambda name, shape, dt=F32: ctx.enter_context(nc.sbuf_tensor(name, shape, dt))
        sem = lambda name: ctx.enter_context(nc.semaphore(name))
        kk = [sb(f"keys{p}", [SPLIT + 1, 2, N], F32R) for p in range(2)]
        vv = [sb(f"values{p}", [P, 2, MT, HD]) for p in range(2)]
        qq = [sb(f"queries{p}", [SPLIT + 1, 2, CH], F32R) for p in range(2)]
        prob = [sb(f"prob{r}", [P, 2, CH]) for r in range(RING)]
        psum = [sb(f"prob_sum{r}", [P, 2, CH]) for r in range(SUM_BUFS)]
        ones = sb("ones", [P, HD])
        bmax = sb("block_max", [P, 2 * NSUB, MB])
        nmax = sb("negated_max", [P, 2 * NSUB], F32R)
        ident_r = sb("ident_r", [P, P], F32R)
        warm = sb("exp_warm", [P, 1])
        num_even = sb("num_even", [2 * HD, CH])
        den_even = sb("den_even", [2 * HD, CH])
        num = sb("num", [2 * HD, CH])
        den = sb("den", [2 * HD, CH])
        dcol = sb("den_col", [P, 2 * CH // P])
        rcol = sb("rec_col", [P, 2 * CH // P])
        rec = sb("rec", [2 * HD, CH])
        fuse = sb("fuse", [2 * HD, CH])
        st = [ctx.enter_context(nc.psum_tensor(f"st{i}", [P, CH], F32)) for i in range(BANKS)]
        mx = [ctx.enter_context(nc.psum_tensor(f"mx{i}", [P, CH], F32)) for i in range(BANKS)]
        acc = ctx.enter_context(nc.psum_tensor("acc", [P, CH], F32))
        dacc = ctx.enter_context(nc.psum_tensor("dacc", [P, CH], F32))

        kv_loaded = [sem(f"kv_loaded{p}") for p in range(2)]
        q_loaded = [sem(f"q_loaded{p}") for p in range(2)]
        consts = sem("constants_ready")
        scores = sem("scores_ready")
        exp_done = sem("exp_done")
        added = sem("group_added")
        v_done = sem("v_products_done")
        sums_done = sem("sum_products_done")
        mx_ready = sem("max_block_ready")
        mx_taken = sem("max_block_taken")
        nmax_ready = sem("negated_max_ready")
        mrow_ready = sem("max_row_ready")
        mrow_set = sem("max_row_set")
        num_half = sem("num_half_ready")
        den_half = sem("den_half_ready")
        num_ready = sem("num_ready")
        den_ready = sem("den_ready")
        den_stored = sem("den_stored")
        dcol_loaded = sem("den_col_loaded")
        rcol_ready = sem("rec_col_ready")
        rcol_stored = sem("rec_col_stored")
        rec_loaded = sem("rec_loaded")
        fuse_ready = sem("fuse_ready")
        fuse_stored = sem("fuse_stored")
        block = ctx.enter_context(nc.Block())

        KV_INC = 16 * 8
        Q_INC = 16 * 6


        @block.sync
        def _(sp):
            sp.sem_inc(den_stored, 16)
            sp.sem_inc(fuse_stored, 16)

            def load_kv(g, p):
                for h in range(2):
                    for r, part in enumerate((0, 1, 0)):
                        row = (g * 2 + part) * 64 + h * HD
                        sp.dma_start(kk[p][r * HD:(r + 1) * HD, h, :].bitcast(F32),
                                     scratch["k"][bass.ds(row, HD), :]).then_inc(kv_loaded[p], 16)
                    sp.dma_start(vv[p][:, h, :, :].rearrange("p m d -> p (m d)"),
                                 scratch["v"][:, bass.ds(g * 2 + h, 1), :].rearrange("p a k -> p (a k)")
                                 ).then_inc(kv_loaded[p], 16)

            def load_q(u, p):
                for h in range(2):
                    for r, part in enumerate((0, 0, 1)):
                        sp.dma_start(qq[p][r * HD:(r + 1) * HD, h, :].bitcast(F32),
                                     scratch["q"][bass.ds(u, 1), part, h * HD:(h + 1) * HD, :].rearrange("a r n -> (a r) n")
                                     ).then_inc(q_loaded[p], 16)

            def finish(v):
                row = scratch["den"][bass.ds(v, 1), :]
                sp.wait_ge(den_ready, v + 2)
                sp.dma_start(row.rearrange("a (h n) -> (a h) n", h=2), den[0:HD + 1:HD, :]).then_inc(den_stored, 16)
                sp.wait_ge(den_stored, 16 * (v + 2))
                sp.dma_start(dcol[:, :], row.rearrange("a (p k) -> (a p) k", p=P)).then_inc(dcol_loaded, 16)
                sp.wait_ge(rcol_ready, v + 1)
                row = scratch["rec"][bass.ds(v, 1), :]
                sp.dma_start(row.rearrange("a (p k) -> (a p) k", p=P), rcol[:, :]).then_inc(rcol_stored, 16)
                sp.wait_ge(rcol_stored, 16 * (v + 1))
                sp.wait_ge(fuse_ready, v + 1)
                for h in range(2):
                    sp.dma_start(rec[HD * h:HD * (h + 1), :], row[:, h * CH:(h + 1) * CH].broadcast_to((HD, CH))
                                 ).then_inc(rec_loaded, 16)
                sp.wait_ge(fuse_ready, v + 2)
                sp.dma_start(scratch["fuse"][bass.ds(v, 1), :, :].rearrange("a r n -> (a r) n"), fuse[:, :]
                             ).then_inc(fuse_stored, 16)

            def step(i, p):
                sp.wait_ge(scores, TILES * (i + 1))
                load_q(i + 2, p)
                finish(i)

            load_q(0, 0)
            load_kv(0, 0)
            load_q(1, 1)
            load_kv(1, 1)

            def steps(g, upto):
                with sp.Fori(0, upto) as c2:
                    for p in range(2):
                        step(g * NCH + c2 * 2 + p, p)

            steps(0, NCH // 2)
            with sp.Fori(1, PAIRS // 2) as g2:
                for odd in range(2):
                    g = g2 * 2 - 1 + odd
                    sp.wait_ge(v_done, QUADS * (g * NCH + 1))
                    load_kv(g + 1, odd)
                    steps(g, NCH // 2)
            steps(PAIRS - 1, NCH // 2 - 1)
            finish(UNITS - 2)
            finish(UNITS - 1)
            sp.wait_ge(fuse_stored, 16 * (UNITS + 1))

        @block.tensor
        def _(pe):
            pe.sem_inc(v_done, QUADS)
            pe.sem_inc(sums_done, SUMS)

            def score(u, p, gp, i):
                pe.wait_ge(exp_done, TILES * (u + 1) + max(i - BANKS + 1, 0))
                s, h = i // 2, i % 2
                nc.tensor.matmul(st[i % BANKS][:, :], kk[gp][:, h, s * P:(s + 1) * P], qq[p][:, h, :],
                                 start=True, stop=True).then_inc(scores, 1)

            def max_block(v, p, gp, j):
                pe.wait_ge(mx_taken, MAXMM * v + j + 1)
                hn, blk = j // MB, j % MB
                h, ns = hn // NSUB, hn % NSUB
                nc.tensor.matmul(mx[j % BANKS][:, :], qq[p][0:SPLIT, h, ns * P:(ns + 1) * P],
                                 kk[gp][0:SPLIT, h, blk * CH:(blk + 1) * CH],
                                 start=True, stop=True).then_inc(mx_ready, 1)

            def max_rows(v):
                pe.wait_ge(nmax_ready, v + 1)
                for h in range(2):
                    for ns in range(NSUB):
                        i = h * NSUB + ns
                        mm = nc.tensor.matmul(mx[h][:, ns * P:(ns + 1) * P], nmax[:, i:i + 1].broadcast_to((P, P)),
                                              ident_r[:, :], start=(ns == 0), stop=True, skip_group_check=True)
                mm.then_inc(mrow_ready, 1)

            def values(u, gp, q):
                if q == 0:
                    pe.wait_ge(num_ready, u + 1)
                pe.wait_ge(exp_done, TILES * (u + 1) + 4 * q + 4)
                for a in range(2):
                    for h in range(2):
                        i = 2 * a + h
                        mm = nc.tensor.matmul(acc[HD * i:HD * (i + 1), :], vv[gp][:, h, 2 * q + a, :],
                                              prob[(2 * q + a) % RING][:, h, :], start=(q == 0), stop=(q == QUADS - 1))
                mm.then_inc(v_done, 1)

            def sums(u, i):
                if i == 0:
                    pe.wait_ge(den_ready, u + 1)
                k = 2 * i
                if k < len(GROUPS):
                    pe.wait_ge(added, ADDS * (u + 1) + GROUP_END[k + 1] - (k + 2))
                    src = [psum[(k + a) % SUM_BUFS] for a in range(2)]
                else:
                    t = GROUP_END[-1] + k - len(GROUPS)
                    pe.wait_ge(exp_done, TILES * (u + 1) + 2 * t + 4)
                    src = [prob[(t + a) % RING] for a in range(2)]
                for a in range(2):
                    for h in range(2):
                        n = 2 * a + h
                        mm = nc.tensor.matmul(dacc[HD * n:HD * (n + 1), :], ones[:, :], src[a][:, h, :],
                                              start=(i == 0), stop=(i == SUMS - 1))
                mm.then_inc(sums_done, 1)

            def unit(u, p, gp, ahead):
                now, reduced, free, block_no = 0.0, 0.0, [0.0] * BANKS, 0

                def pace(t, early=0.0):
                    nonlocal now, reduced, block_no
                    now += t
                    while ahead and block_no < MAXMM and free[block_no % BANKS] <= now + early:
                        max_block(u + 1, 1 - p, ahead[0], block_no)
                        now = max(now, free[block_no % BANKS]) + T_ONE
                        reduced = max(now + T_SEEN, reduced) + T_REDUCE + T_BETWEEN.get(block_no, 0.0)
                        free[block_no % BANKS] = reduced + T_HANDOVER
                        block_no += 1

                for w, value in (ahead[1] if ahead else ()):
                    pe.wait_ge(w, value)
                for s in range(MT - 1):
                    for i in range(2 * s + BANKS, min(2 * s + BANKS + 2, TILES)):
                        score(u, p, gp, i)
                        pace(T_ONE)
                    if s % 2 and s >= V_LAG:
                        values(u, gp, (s - V_LAG) // 2)
                        pace(T_QUAD)
                    if s in SUM_STEP:
                        sums(u, SUM_STEP.index(s))
                        pace(T_QUAD)
                if ahead:
                    for j in range(block_no, MAXMM):
                        max_block(u + 1, 1 - p, ahead[0], j)
                values(u, gp, QUADS - 2)
                sums(u, SUM_ORDER[-3])
                if ahead:
                    max_rows(u + 1)
                sums(u, SUM_ORDER[-2])
                values(u, gp, QUADS - 1)
                if ahead:
                    pe.wait_ge(mrow_set, 2 * (u + 1) + 2)
                    for i in range(BANKS):
                        score(u + 1, 1 - p, ahead[0], i)
                sums(u, SUM_ORDER[-1])

            def pair(g2, gp, more):
                g = g2 * 2 + gp
                nq = lambda c2: Q_INC * (g * (NCH // 2) + c2 + 1)
                with pe.Fori(0, NCH // 2 - 1) as c2:
                    unit(g * NCH + c2 * 2, 0, gp, (gp, [(q_loaded[1], nq(c2))]))
                    unit(g * NCH + c2 * 2 + 1, 1, gp, (gp, [(q_loaded[0], nq(c2 + 1))]))
                c2 = NCH // 2 - 1
                unit(g * NCH + c2 * 2, 0, gp, (gp, [(q_loaded[1], nq(c2))]))
                nk = KV_INC * (g2 + 1 + gp)
                unit(g * NCH + c2 * 2 + 1, 1, gp,
                     (1 - gp, [(q_loaded[0], nq(c2 + 1)), (kv_loaded[1 - gp], nk)]) if more else None)

            pe.wait_ge(consts, 4)
            pe.wait_ge(q_loaded[0], Q_INC)
            pe.wait_ge(kv_loaded[0], KV_INC)
            for j in range(MAXMM):
                max_block(0, 0, 0, j)
            max_rows(0)
            pe.wait_ge(mrow_set, 2)
            for i in range(BANKS):
                score(0, 0, 0, i)
            with pe.Fori(0, PAIRS // 2 - 1) as g2:
                pair(g2, 0, True)
                pair(g2, 1, True)
            pair(PAIRS // 2 - 1, 0, True)
            pair(PAIRS // 2 - 1, 1, False)

        @block.scalar
        def _(act):
            def rows(v, p):
                act.wait_ge(mrow_ready, v + 1)
                nc.scalar.copy(qq[p][SPLIT:SPLIT + 1, 0, :], mx[0][SPLIT:SPLIT + 1, :]).then_inc(mrow_set, 1)

            def halves(v):
                act.wait_ge(num_ready, v + 1)
                act.wait_ge(v_done, QUADS * (v + 2))
                nc.scalar.copy(num_even[:, :], acc[0:2 * HD, :]).then_inc(num_half, 1)
                act.wait_ge(den_ready, v + 1)
                act.wait_ge(sums_done, SUMS * (v + 2))
                nc.scalar.copy(den_even[:, :], dacc[0:2 * HD, :]).then_inc(den_half, 1)

            def unit(u, p, prev=True, ahead=True):
                for i in range(TILES):
                    s, h = i // 2, i % 2
                    act.wait_ge(scores, TILES * u + i + 1)
                    if h == 0:
                        if s >= RING:
                            act.wait_ge(v_done, QUADS * (u + 1) + (s - RING) // 2 + 1)
                            k = sum(e <= s - RING for e in GROUP_END)
                            act.wait_ge(added, ADDS * (u + 1) + GROUP_END[k] - (k + 1))
                        elif s >= RING - PLAIN:
                            act.wait_ge(v_done, QUADS * (u + 1) - (RING - 1 - s) // 2)
                            act.wait_ge(sums_done, SUMS * u + SUM_COUNT[SUMS - 1 - (RING - 1 - s) // 2])
                        else:
                            act.wait_ge(v_done, QUADS * (u + 1) - (RING - 1 - s) // 2)
                            act.wait_ge(added, ADDS * (u + 1))
                    nc.scalar.activation(prob[s % RING][:, h, :], st[i % BANKS][:, :], ACT.Exp).then_inc(exp_done, 1)
                    if i == BANKS - 1 and prev:
                        halves(u - 1)
                if ahead:
                    rows(u + 1, 1 - p)

            act.sem_inc(exp_done, TILES)
            act.wait_ge(consts, 4)
            nc.scalar.activation(warm[:, :], ones[:, 0:1], ACT.Exp)
            rows(0, 0)
            unit(0, 0, prev=False)
            with act.Fori(0, UNITS // 2 - 1) as u2:
                unit(u2 * 2 + 1, 1)
                unit(u2 * 2 + 2, 0)
            unit(UNITS - 1, 1, ahead=False)
            halves(UNITS - 1)

        @block.vector
        def _(dve):
            dve.sem_inc(mx_taken, BANKS)
            dve.sem_inc(num_ready, 1)
            dve.sem_inc(den_ready, 1)

            def take_num(v):
                dve.wait_ge(num_half, v + 1)
                dve.wait_ge(fuse_ready, v + 1)
                nc.vector.tensor_tensor(num[:, :], acc[2 * HD:4 * HD, :], num_even[:, :], ALU.add).then_inc(num_ready, 1)

            def take_den(v):
                dve.wait_ge(den_half, v + 1)
                dve.wait_ge(den_stored, 16 * (v + 1))
                nc.vector.tensor_tensor(den[:, :], dacc[2 * HD:4 * HD, :], den_even[:, :], ALU.add).then_inc(den_ready, 1)

            def invert(v):
                dve.wait_ge(dcol_loaded, 16 * (v + 1))
                nc.vector.reciprocal(rcol[:, :], dcol[:, :]).then_inc(rcol_ready, 1)

            def maxima(v, p, prev):
                for j in range(MAXMM):
                    dve.wait_ge(mx_ready, MAXMM * v + j + 1)
                    nc.vector.tensor_reduce(bmax[:, j // MB, j % MB:j % MB + 1], mx[j % BANKS][:, :], AX.X,
                                            ALU.max).then_inc(mx_taken, 1)
                    if prev is not None:
                        if j == TAKE_NUM:
                            take_num(prev)
                        if j == TAKE_DEN:
                            take_den(prev)
                        if j == INVERT:
                            invert(prev)
                dve.wait_ge(mx_taken, MAXMM * v + MAXMM + BANKS)
                nc.vector.tensor_reduce(nmax[:, :], bmax[:, :, :], AX.X, ALU.max, negate=True).then_inc(nmax_ready, 1)
                dve.wait_ge(mrow_ready, v + 1)
                nc.vector.tensor_copy(qq[p][SPLIT:SPLIT + 1, 1, :], mx[1][SPLIT:SPLIT + 1, :]).then_inc(mrow_set, 1)

            for p in range(2):
                nc.vector.memset(kk[p][SPLIT:SPLIT + 1, :, :].bitcast(F32), 1.0).then_inc(consts, 1)
            nc.vector.memset(ones[:, :], 1.0).then_inc(consts, 1)
            nc.vector.tensor_copy(ident_r[:, :], keep["ident"][:, :]).then_inc(consts, 1)
            maxima(0, 0, None)
            maxima(1, 1, None)
            with dve.Fori(1, UNITS // 2) as v2:
                maxima(v2 * 2, 0, v2 * 2 - 2)
                maxima(v2 * 2 + 1, 1, v2 * 2 - 1)
            for v in (UNITS - 2, UNITS - 1):
                take_num(v)
                take_den(v)
                invert(v)

        @block.gpsimd
        def _(pool):
            pool.sem_inc(added, ADDS)
            pool.sem_inc(fuse_ready, 1)

            def scale(v):
                pool.wait_ge(num_ready, v + 2)
                pool.wait_ge(rec_loaded, 32 * (v + 1))
                pool.wait_ge(fuse_stored, 16 * (v + 1))
                nc.gpsimd.tensor_tensor(fuse[:, :], num[:, :], rec[:, :], ALU.mult).then_inc(fuse_ready, 1)

            def unit(u, prev=True):
                for k, size in enumerate(GROUPS):
                    first = GROUP_END[k] - size
                    dst = psum[k % SUM_BUFS]
                    if k >= SUM_BUFS:
                        pool.wait_ge(sums_done, SUMS * (u + 1) + SUM_COUNT[(k - SUM_BUFS) // 2])
                    else:
                        pool.wait_ge(sums_done, SUMS * u + SUM_COUNT[(len(GROUPS) - SUM_BUFS + k) // 2])
                    for i in range(1, size):
                        n = ADDS * (u + 1) + first - k + i
                        pool.wait_ge(exp_done, TILES * (u + 1) + 2 * (first + i) + 2)
                        if i > 1:
                            pool.wait_ge(added, n - 1)
                        a = prob[first % RING] if i == 1 else dst
                        nc.gpsimd.tensor_tensor(dst[:, :, :], a[:, :, :], prob[(first + i) % RING][:, :, :],
                                                ALU.add).then_inc(added, 1)
                    if k == 5 and prev:
                        scale(u - 1)

            unit(0, prev=False)
            with pool.Fori(1, UNITS) as u:
                unit(u)
            scale(UNITS - 1)


def image_phase(nc, dram, keep, scratch, out):
    with ExitStack() as ctx:
        sb = lambda name, shape, dt=F32: ctx.enter_context(nc.sbuf_tensor(name, shape, dt))
        sem = lambda name: ctx.enter_context(nc.semaphore(name))
        xf = [sb(f"xf{p}", [P, 2 * CT, CH]) for p in range(2)]
        m32 = sb("m32", [P, 32, 32])
        q32 = sb("q32", [P, 32, 32])
        m64 = sb("m64", [P, 32, WW])
        q64 = sb("q64", [P, 32, WW])
        mask = sb("mask", [P, HH, WW])
        diff = sb("diff", [P, CT, CH])
        y = sb("y", [P, CT, PR, PW])
        o1 = sb("o1", [P, CT, PR, PW])
        edge = [sb(f"edge{p}", [P, CT, CH]) for p in range(2)]
        dw = sb("dw", [P, CT, N])
        ysum = sb("ysum", [P, CT])
        hid = sb("hid", [HID, 1])
        nexp = sb("nexp", [P, CT])
        gate1 = sb("gate1", [P, CT])
        gate = sb("gate", [P, CT])
        fus = sb("fus", [P, CT, C])
        last = [sb(f"last{p}", [P, CT, CH]) for p in range(2)]
        bank = [ctx.enter_context(nc.psum_tensor(f"bank{i}", [P, CH], F32)) for i in range(8)]

        mask_loaded = sem("mask_loaded")
        mstep = sem("mask_step")
        xf_loaded = [sem(f"xf_loaded{p}") for p in range(2)]
        borders = sem("borders_zeroed")
        hybrid = sem("hybrid_ready")
        diffed = sem("diff_ready")
        masked = sem("masked_ready")
        y_ready = sem("y_ready")
        sum_ready = sem("sum_ready")
        hid_mm = sem("hidden_product")
        hid_ready = sem("hidden_ready")
        z_ready = sem("gate_product")
        nexp_ready = sem("gate_exp")
        gstep = sem("gate_step")
        edge_mm = sem("edge_product")
        edge_ready = sem("edge_ready")
        fus_mm = sem("fusion_product")
        o1_ready = sem("o1_ready")
        dwstep = sem("deform_step")
        bal_mm = sem("balance_product")
        last_ready = sem("last_ready")
        res_ready = sem("result_ready")
        stored = [sem(f"stored{p}") for p in range(2)]
        block = ctx.enter_context(nc.Block())

        XF_INC = 16 * (1 + HEADS // 2)
        x_rows = dram["x"].rearrange("b (t p) h w -> p (b t) (h w)", p=P)
        out_rows = out.rearrange("b (t p) h w -> p (b t) (h w)", p=P)

        def inner(t, ot, c, rows=ROWS, dy=1, dx=1):
            return t[:, ot, bass.ds(c * ROWS + dy, rows), dx:dx + WW]

        as_rows = lambda ap: ap.rearrange("p (r w) -> p r w", w=WW)

        @block.sync
        def _(sp):
            with sp.Fori(0, B) as b:
                sp.wait_ge(y_ready, 2 * NCH * b)
                sp.dma_start(m32[:, :, :].rearrange("p h w -> p (h w)"),
                             dram["mask"].rearrange("b a h w -> (b a) (h w)")[bass.ds(b, 1), :].broadcast_to((P, 1024))
                             ).then_inc(mask_loaded, 16)
                with sp.Fori(0, NCH // 2) as c2:
                    for p in range(2):
                        n = b * (NCH // 2) + c2
                        c = c2 * 2 + p
                        if p == 0:
                            sp.wait_ge(y_ready, 2 * NCH * b + 4 * c2)
                        sp.dma_start(xf[p][:, 0:CT, :], x_rows[:, bass.ds(b * CT, CT), bass.ds(c * CH, CH)]
                                     ).then_inc(xf_loaded[p], 16)
                        for g in range(HEADS // 2):
                            sp.dma_start(xf[p][64 * (g % 2):64 * (g % 2) + 64, CT + g // 2, :],
                                         scratch["fuse"][bass.ds((b * (HEADS // 2) + g) * NCH + c, 1), :, :]
                                         .rearrange("a r n -> (a r) n")).then_inc(xf_loaded[p], 16)
                with sp.Fori(0, NCH // 2) as c2:
                    for p in range(2):
                        c = c2 * 2 + p
                        sp.wait_ge(res_ready, 2 * (b * NCH + c) + 2)
                        sp.dma_start(out_rows[:, bass.ds(b * CT, CT), bass.ds(c * CH, CH)], last[p][:, :, :]
                                     ).then_inc(stored[p], 16)
            for p in range(2):
                sp.wait_ge(stored[p], 16 * B * NCH // 2)

        @block.tensor
        def _(pe):
            pe.wait_ge(borders, 2)
            with pe.Fori(0, B) as b:
                with pe.Fori(0, NCH // 2) as c2:
                    for p in range(2):
                        n = b * NCH + c2 * 2 + p
                        pe.wait_ge(xf_loaded[p], XF_INC * (b * (NCH // 2) + c2) + XF_INC)
                        if p == 0:
                            pe.wait_ge(diffed, 2 * n)
                        for ot in range(CT):
                            for kt in range(2 * CT):
                                mm = nc.tensor.matmul(bank[2 * p + ot][:, :], keep["wf"][:, kt, ot * P:(ot + 1) * P],
                                                      xf[p][:, kt, :], start=(kt == 0), stop=(kt == 2 * CT - 1))
                            mm.then_inc(hybrid, 1)
                pe.wait_ge(sum_ready, 2 * b + 2)
                for kt in range(CT):
                    mm = nc.tensor.matmul(bank[4][0:HID, 0:1], keep["fc1"][:, kt, :], ysum[:, kt:kt + 1],
                                          start=(kt == 0), stop=(kt == CT - 1))
                mm.then_inc(hid_mm, 1)
                pe.wait_ge(hid_ready, b + 1)
                for ot in range(CT):
                    mm = nc.tensor.matmul(bank[5][:, ot:ot + 1], keep["fc2"][:, ot * P:(ot + 1) * P], hid[:, :],
                                          start=(ot == 0), stop=True, skip_group_check=True)
                mm.then_inc(z_ready, 1)
                with pe.Fori(0, NCH // 2) as c2:
                    for p in range(2):
                        n = b * NCH + c2 * 2 + p
                        c = c2 * 2 + p
                        pe.wait_ge(gstep, 4 * b + 4)
                        pe.wait_ge(edge_ready, 2 * n)
                        for ct in range(CT):
                            for k in range(TAPS):
                                mm = nc.tensor.matmul(as_rows(bank[ct][:, :]), keep["diag"][:, ct, k, :],
                                                      inner(y, ct, c, dy=k // 3, dx=k % 3),
                                                      start=(k == 0), stop=(k == TAPS - 1))
                            mm.then_inc(edge_mm, 1)
                        pe.wait_ge(o1_ready, 2 * n)
                        pe.wait_ge(edge_ready, 2 * n + 2)
                        for ot in range(CT):
                            for kt in range(CT):
                                nc.tensor.matmul(as_rows(bank[2 + ot][:, :]), fus[:, kt, ot * P:(ot + 1) * P],
                                                 inner(y, kt, c), start=(kt == 0), stop=False)
                            for kt in range(CT):
                                mm = nc.tensor.matmul(as_rows(bank[2 + ot][:, :]),
                                                      keep["fu"][:, CT + kt, ot * P:(ot + 1) * P],
                                                      as_rows(edge[p][:, kt, :]), start=False, stop=(kt == CT - 1))
                            mm.then_inc(fus_mm, 1)
                with pe.Fori(0, NCH // 2) as c2:
                    for p in range(2):
                        n = b * NCH + c2 * 2 + p
                        c = c2 * 2 + p
                        if p == 0:
                            pe.wait_ge(last_ready, 2 * n)
                        pe.wait_ge(dwstep, CT * TAPS * (n + 1))
                        for ot in range(CT):
                            for kt in range(CT):
                                mm = nc.tensor.matmul(bank[4 + 2 * p + ot][:, :], keep["ba"][:, kt, ot * P:(ot + 1) * P],
                                                      dw[:, kt, bass.ds(c * CH, CH)],
                                                      start=(kt == 0), stop=(kt == CT - 1))
                            mm.then_inc(bal_mm, 1)

        @block.scalar
        def _(act):
            with act.Fori(0, B) as b:
                act.wait_ge(hid_mm, b + 1)
                nc.scalar.activation(hid[:, :], bank[4][0:HID, 0:1], ACT.Relu, scale=1.0 / N).then_inc(hid_ready, 1)
                act.wait_ge(z_ready, b + 1)
                nc.scalar.activation(nexp[:, :], bank[5][:, 0:CT], ACT.Exp, scale=-1.0).then_inc(nexp_ready, 1)
                with act.Fori(0, NCH // 2) as c2:
                    for p in range(2):
                        n = b * NCH + c2 * 2 + p
                        c = c2 * 2 + p
                        for ct in range(CT):
                            act.wait_ge(edge_mm, 2 * n + ct + 1)
                            nc.scalar.activation(edge[p][:, ct, :], bank[ct][:, :], ACT.Relu,
                                                 scale=keep["nscale"][:, 0, ct:ct + 1],
                                                 bias=keep["nshift"][:, 0, ct:ct + 1]).then_inc(edge_ready, 1)
                        for ot in range(CT):
                            act.wait_ge(fus_mm, 2 * n + ot + 1)
                            nc.scalar.activation(inner(o1, ot, c), as_rows(bank[2 + ot][:, :]), ACT.Identity,
                                                 scale=keep["nscale"][:, 1, ot:ot + 1],
                                                 bias=keep["nshift"][:, 1, ot:ot + 1]).then_inc(o1_ready, 1)
                with act.Fori(0, NCH // 2) as c2:
                    for p in range(2):
                        n = b * NCH + c2 * 2 + p
                        act.wait_ge(stored[p], 16 * (b * (NCH // 2) + c2))
                        for ot in range(CT):
                            act.wait_ge(bal_mm, 2 * n + ot + 1)
                            nc.scalar.activation(last[p][:, ot, :], bank[4 + 2 * p + ot][:, :], ACT.Identity,
                                                 scale=keep["nscale"][:, 2, ot:ot + 1],
                                                 bias=keep["nshift"][:, 2, ot:ot + 1]).then_inc(last_ready, 1)

        @block.gpsimd
        def _(pool):
            nc.gpsimd.memset(y[:, :, :, :].rearrange("p t r w -> p (t r w)"), 0.0).then_inc(borders, 1)
            nc.gpsimd.memset(o1[:, :, :, :].rearrange("p t r w -> p (t r w)"), 0.0).then_inc(borders, 1)

        @block.vector
        def _(dve):
            NM = 10

            def upsample(b):
                n = [0]

                def link(ins):
                    n[0] += 1
                    ins.then_inc(mstep, 1)
                    if n[0] < NM:
                        dve.wait_ge(mstep, b * NM + n[0])

                link(nc.vector.tensor_scalar(q32[:, :, :], m32[:, :, :], 0.25, None, ALU.mult))
                cols = m64[:, :, :].rearrange("p h (w a) -> p h w a", a=2)
                link(nc.vector.scalar_tensor_tensor(out=cols[:, :, 1:32, 0], in0=m32[:, :, 1:32], scalar=0.75,
                                                    in1=q32[:, :, 0:31], op0=ALU.mult, op1=ALU.add))
                link(nc.vector.scalar_tensor_tensor(out=cols[:, :, 0:31, 1], in0=m32[:, :, 0:31], scalar=0.75,
                                                    in1=q32[:, :, 1:32], op0=ALU.mult, op1=ALU.add))
                link(nc.vector.tensor_copy(cols[:, :, 0, 0], m32[:, :, 0]))
                link(nc.vector.tensor_copy(cols[:, :, 31, 1], m32[:, :, 31]))
                link(nc.vector.tensor_scalar(q64[:, :, :], m64[:, :, :], 0.25, None, ALU.mult))
                rows = mask[:, :, :].rearrange("p (h a) w -> p h a w", a=2)
                link(nc.vector.scalar_tensor_tensor(out=rows[:, 1:32, 0, :], in0=m64[:, 1:32, :], scalar=0.75,
                                                    in1=q64[:, 0:31, :], op0=ALU.mult, op1=ALU.add))
                link(nc.vector.scalar_tensor_tensor(out=rows[:, 0:31, 1, :], in0=m64[:, 0:31, :], scalar=0.75,
                                                    in1=q64[:, 1:32, :], op0=ALU.mult, op1=ALU.add))
                link(nc.vector.tensor_copy(rows[:, 0, 0, :], m64[:, 0, :]))
                link(nc.vector.tensor_copy(rows[:, 31, 1, :], m64[:, 31, :]))

            dve.wait_ge(borders, 2)
            with dve.Fori(0, B) as b:
                dve.wait_ge(mask_loaded, 16 * b + 16)
                upsample(b)
                with dve.Fori(0, NCH // 2) as c2:
                    for p in range(2):
                        n = b * NCH + c2 * 2 + p
                        c = c2 * 2 + p
                        for ot in range(CT):
                            dve.wait_ge(hybrid, 2 * n + ot + 1)
                            dve.wait_ge(y_ready, 2 * n)
                            nc.vector.scalar_tensor_tensor(
                                out=diff[:, ot, :], in0=bank[2 * p + ot][:, :],
                                scalar=keep["vec"][:, VEC.index("bf"), ot:ot + 1], in1=xf[p][:, ot, :],
                                op0=ALU.add, op1=ALU.subtract).then_inc(diffed, 1)
                        for ot in range(CT):
                            dve.wait_ge(diffed, 2 * n + ot + 1)
                            dve.wait_ge(mstep, NM * b + NM)
                            nc.vector.tensor_tensor(as_rows(diff[:, ot, :]), as_rows(diff[:, ot, :]),
                                                    mask[:, bass.ds(c * ROWS, ROWS), :], ALU.mult).then_inc(masked, 1)
                        for ot in range(CT):
                            dve.wait_ge(masked, 2 * n + ot + 1)
                            nc.vector.tensor_tensor(inner(y, ot, c), as_rows(diff[:, ot, :]),
                                                    as_rows(xf[p][:, ot, :]), ALU.add).then_inc(y_ready, 1)
                dve.wait_ge(y_ready, 2 * NCH * (b + 1))
                for ct in range(CT):
                    nc.vector.tensor_reduce(ysum[:, ct:ct + 1], y[:, ct, 1:1 + HH, 1:1 + WW], AX.XY,
                                            ALU.add).then_inc(sum_ready, 1)
                dve.wait_ge(nexp_ready, b + 1)
                nc.vector.tensor_scalar(gate1[:, :], nexp[:, :], 1.0, None, ALU.add).then_inc(gstep, 1)
                dve.wait_ge(gstep, 4 * b + 1)
                nc.vector.reciprocal(gate[:, :], gate1[:, :]).then_inc(gstep, 1)
                dve.wait_ge(gstep, 4 * b + 2)
                for kt in range(CT):
                    nc.vector.tensor_scalar(fus[:, kt, :], keep["fu"][:, kt, :], gate[:, kt:kt + 1], None,
                                            ALU.mult).then_inc(gstep, 1)

                def deform(c, last_c):
                    n = b * NCH + c
                    dve.wait_ge(o1_ready, 2 * n + (2 if last_c else 4))
                    for k in range(TAPS):
                        for ct in range(CT):
                            dst = as_rows(dw[:, ct, bass.ds(c * CH, CH)])
                            src = inner(o1, ct, c, dy=k // 3, dx=k % 3)
                            w = keep["dtaps"][:, ct, k:k + 1]
                            at = CT * TAPS * n + CT * k + ct
                            if k == 0:
                                ins = nc.vector.tensor_scalar(dst, src, w, None, ALU.mult)
                            else:
                                dve.wait_ge(dwstep, at - 1)
                                ins = nc.vector.scalar_tensor_tensor(out=dst, in0=src, scalar=w, in1=dst,
                                                                     op0=ALU.mult, op1=ALU.add)
                            ins.then_inc(dwstep, 1)

                with dve.Fori(0, NCH - 1) as c:
                    deform(c, False)
                deform(NCH - 1, True)
                with dve.Fori(0, NCH // 2) as c2:
                    for p in range(2):
                        c = c2 * 2 + p
                        for ot in range(CT):
                            dve.wait_ge(last_ready, 2 * (b * NCH + c) + ot + 1)
                            nc.vector.tensor_tensor(as_rows(last[p][:, ot, :]), as_rows(last[p][:, ot, :]),
                                                    inner(y, ot, c), ALU.mult).then_inc(res_ready, 1)


def build(nc, dram, out):
    with ExitStack() as ctx:
        sb = lambda name, shape: ctx.enter_context(nc.sbuf_tensor(name, shape, F32))
        keep = {
            "ident": sb("ident", [P, P]),
            "vec": sb("vec", [P, NVEC, CT]),
            "bqs": sb("bqs", [P, 2, CT]),
            "bv": sb("bv_rows", [P, C]),
            "nscale": sb("nscale", [P, 3, CT]),
            "nshift": sb("nshift", [P, 3, CT]),
            "dtaps": sb("dtaps", [P, CT, TAPS]),
            "diag": sb("diag", [P, CT, TAPS, P]),
            "fc1": sb("fc1T", [P, CT, HID]),
            "fc2": sb("fc2T", [HID, C]),
        }
        for w, ots, kts in WEIGHTS:
            keep[w] = sb(f"{w}T", [P, kts, ots * P])
        scratch = {
            "q": nc.dram_tensor("q_scratch", [UNITS, 2, 64, CH], F32).ap(),
            "k": nc.dram_tensor("k_scratch", [PAIRS * 2 * 64, N], F32).ap(),
            "v": nc.dram_tensor("v_scratch", [P, B * HEADS, MT * HD], F32).ap(),
            "den": nc.dram_tensor("den_scratch", [UNITS, 2 * CH], F32).ap(),
            "rec": nc.dram_tensor("rec_scratch", [UNITS, 2 * CH], F32).ap(),
            "fuse": nc.dram_tensor("fuse_scratch", [UNITS, 2 * HD, CH], F32).ap(),
        }
        setup_phase(nc, dram, keep)
        project_phase(nc, dram, keep, scratch)
        attention_phase(nc, keep, scratch)
        image_phase(nc, dram, keep, scratch, out)


_INS = {
    "x": "x", "mask": "L0_conv_mask", "wq": "L0_conv_Wq", "bq": "L0_conv_bq", "wk": "L0_conv_Wk", "bk": "L0_conv_bk",
    "wv": "L0_conv_Wv", "bv": "L0_conv_bv", "wf": "L0_conv_Wf", "bf": "L0_conv_bf",
    "edge_w": "L1_conv_edge_w", "edge_gamma": "L1_conv_edge_gamma", "edge_beta": "L1_conv_edge_beta",
    "edge_mean": "L1_conv_edge_mean", "edge_var": "L1_conv_edge_var", "fc1": "L1_conv_fc1_w", "fc2": "L1_conv_fc2_w",
    "fu": "L1_conv_fusion_w", "fusion_b": "L1_conv_fusion_b", "bn1_gamma": "L1_conv_bn1_gamma",
    "bn1_beta": "L1_conv_bn1_beta", "bn1_mean": "L1_conv_bn1_mean", "bn1_var": "L1_conv_bn1_var",
    "deform_w": "L1_conv_deform_w", "ba": "L1_conv_balance_w", "balance_b": "L1_conv_balance_b",
    "bn2_gamma": "L1_conv_bn2_gamma", "bn2_beta": "L1_conv_bn2_beta", "bn2_mean": "L1_conv_bn2_mean",
    "bn2_var": "L1_conv_bn2_var",
}


def kernel(**inputs):
    import numpy as _np
    import concourse.bacc as _bacc
    from concourse import mybir as _mybir
    from concourse.bass_utils import run_bass_kernel_spmd as _run

    nc = _bacc.Bacc("TRN2", target_bir_lowering=False, num_devices=1)
    arrays, dram = {}, {}
    for short, name in _INS.items():
        a = _np.ascontiguousarray(inputs[name])
        arrays[f"in_{name}"] = a
        dram[short] = nc.dram_tensor(f"in_{name}", a.shape, _mybir.dt.from_np(a.dtype), kind="ExternalInput").ap()
    out = nc.dram_tensor("out_dram", (B, C, HH, WW), F32, kind="ExternalOutput").ap()
    build(nc, dram, out)
    r = _run(nc, [arrays], core_ids=[0])
    return r.results[0]["out_dram"]
```

```python
from contextlib import ExitStack

import concourse.bass as bass
from concourse import mybir

F32 = mybir.dt.float32
F32R = mybir.dt.float32r
ALU = mybir.AluOpType
ACT = mybir.ActivationFunctionType
AX = mybir.AxisListType

P = 128
B, C, HH, WW = 2, 256, 64, 64
N = HH * WW
CT = C // P
HEADS = 8
HD = C // HEADS
QS = float(HD) ** -0.5
CH = 512
NCH = N // CH
MT = N // P
PAIRS = B * HEADS // 2
UNITS = PAIRS * NCH
ROWS = CH // WW
PW = WW + 2
PR = HH + 2
SPLIT = 3 * HD
NSUB = CH // P
MB = N // CH
MAXMM = 2 * NSUB * MB
EPS = 1e-5
HID = C // 16
TAPS = 9
NM = 11

VEC = ["bq", "bk", "bf", "edge_gamma", "edge_beta", "edge_mean", "edge_var", "fusion_b",
       "bn1_gamma", "bn1_beta", "bn1_mean", "bn1_var", "balance_b",
       "bn2_gamma", "bn2_beta", "bn2_mean", "bn2_var"]
NVEC = len(VEC)
NORMS = [("edge", None), ("bn1", "fusion_b"), ("bn2", "balance_b")]
WEIGHTS = [("wq", CT, CT), ("wk", CT, CT), ("wv", CT, CT), ("wf", CT, 2 * CT), ("fu", CT, 2 * CT), ("ba", CT, CT)]


def setup_phase(nc, dram, keep):
    blocks = [(w, ot, kt) for w, ots, kts in WEIGHTS for ot in range(ots) for kt in range(kts)]
    with ExitStack() as ctx:
        sb = lambda name, shape, dt=F32: ctx.enter_context(nc.sbuf_tensor(name, shape, dt))
        sem = lambda name: ctx.enter_context(nc.semaphore(name))
        raw = {w: sb(f"raw_{w}", [P, ots, kts * P]) for w, ots, kts in WEIGHTS}
        raw_fc1 = sb("raw_fc1", [HID, C])
        raw_fc2 = sb("raw_fc2", [P, CT, HID])
        raw_vec = sb("raw_vec", [NVEC * CT, P])
        vec = keep["vec"]
        root = sb("root", [P, 3 * CT])
        vare = sb("vare", [P, 3 * CT])
        inv = sb("inv", [P, 3 * CT])
        t0 = sb("t0", [P, 3 * CT])
        t1 = sb("t1", [P, 3 * CT])
        ps = [ctx.enter_context(nc.psum_tensor(f"ps{i}", [P, CH], F32)) for i in range(4)]

        loaded = sem("weights_loaded")
        ident_zero = sem("ident_zeroed")
        ident_ready = sem("ident_ready")
        turned = sem("weights_turned")
        copied = sem("turned_copied")
        var_ready = sem("variance_ready")
        root_ready = sem("root_ready")
        step = sem("dve_setup_step")
        done = sem("setup_done")
        block = ctx.enter_context(nc.Block())
        n_loads = len(WEIGHTS) + 2 + NVEC + 3

        @block.sync
        def _(sp):
            for w, ots, kts in WEIGHTS:
                sp.dma_start(raw[w][:, :, :], dram[w].rearrange("(t p) k -> p t k", p=P)).then_inc(loaded, 16)
            sp.dma_start(raw_fc1[:, :], dram["fc1"]).then_inc(loaded, 16)
            sp.dma_start(raw_fc2[:, :, :], dram["fc2"].rearrange("(t p) k -> p t k", p=P)).then_inc(loaded, 16)
            for i, v in enumerate(VEC):
                sp.dma_start(raw_vec[CT * i:CT * i + CT, :], dram[v].rearrange("(t p) -> t p", p=P)).then_inc(loaded, 16)
            sp.dma_start(keep["etaps"][:, :, :], dram["edge_w"].rearrange("(t p) a h w -> p t (a h w)", p=P)).then_inc(loaded, 16)
            sp.dma_start(keep["dtaps"][:, :, :],
                         dram["deform_w"].rearrange("(t p) a h w -> p t (a h w)", p=P)).then_inc(loaded, 16)
            sp.dma_start(keep["bv"][:, :], dram["bv"].rearrange("(a k) -> a k", a=1).broadcast_to((P, C))).then_inc(loaded, 16)

        @block.gpsimd
        def _(pool):
            ident = keep["ident"]
            nc.gpsimd.memset(ident[:, :], 0.0).then_inc(ident_zero, 1)
            pool.wait_ge(ident_zero, 1)
            nc.gpsimd.affine_select(out=ident[:, :], in_=ident[:, :], compare_op=ALU.not_equal, fill=1.0,
                                    base=0, pattern=[[-1, P]], channel_multiplier=1).then_inc(ident_ready, 1)

        n_turned = 1 + len(blocks) + 2 * CT

        def turned_io(i):
            if i == 0:
                return raw_vec[:, :], vec[:, :, :].rearrange("p i t -> p (i t)"), NVEC * CT, P
            i -= 1
            if i < len(blocks):
                w, ot, kt = blocks[i]
                return raw[w][:, ot, kt * P:(kt + 1) * P], keep[w][:, kt, ot * P:(ot + 1) * P], P, P
            t = i - len(blocks)
            if t < CT:
                return raw_fc1[:, t * P:(t + 1) * P], keep["fc1"][:, t, :], HID, P
            return raw_fc2[:, t - CT, :], keep["fc2"][:, (t - CT) * P:(t - CT + 1) * P], P, HID

        @block.tensor
        def _(pe):
            pe.wait_ge(ident_ready, 1)
            pe.wait_ge(loaded, 16 * n_loads)
            for i in range(n_turned):
                src, _, rows, cols = turned_io(i)
                if i >= 4:
                    pe.wait_ge(copied, i - 3)
                nc.tensor.transpose(ps[i % 4][0:cols, 0:rows], src, keep["ident"][0:rows, 0:rows]).then_inc(turned, 1)

        @block.scalar
        def _(act):
            act.wait_ge(var_ready, 1)
            nc.scalar.activation(root[:, :], vare[:, :], ACT.Sqrt).then_inc(root_ready, 1)

        @block.vector
        def _(dve):
            n = [0]

            def link(ins):
                n[0] += 1
                ins.then_inc(step, 1)
                dve.wait_ge(step, n[0])

            def take(i):
                _, dst, rows, cols = turned_io(i)
                dve.wait_ge(turned, i + 1)
                nc.vector.tensor_copy(dst, ps[i % 4][0:cols, 0:rows]).then_inc(copied, 1)

            take(0)
            dve.wait_ge(copied, 1)
            col = lambda name: vec[:, VEC.index(name), :]
            link(nc.vector.tensor_scalar(keep["bqs"][:, 0, :], col("bq"), QS, None, ALU.mult))
            link(nc.vector.tensor_copy(keep["bqs"][:, 1, :], col("bk")))
            for j, (norm, _) in enumerate(NORMS):
                link(nc.vector.tensor_scalar(vare[:, CT * j:CT * j + CT], col(f"{norm}_var"), EPS, None, ALU.add))
            nc.vector.memset(t0[:, :], 1.5).then_inc(var_ready, 1)
            dve.wait_ge(root_ready, 1)
            link(nc.vector.reciprocal(inv[:, :], root[:, :]))
            link(nc.vector.tensor_tensor(t0[:, :], inv[:, :], inv[:, :], ALU.mult))
            link(nc.vector.tensor_tensor(t1[:, :], t0[:, :], vare[:, :], ALU.mult))
            link(nc.vector.tensor_scalar(t0[:, :], t1[:, :], -0.5, 1.5, ALU.mult, ALU.add))
            link(nc.vector.tensor_tensor(t1[:, :], t0[:, :], inv[:, :], ALU.mult))
            for j, (norm, bias) in enumerate(NORMS):
                s = keep["nscale"][:, j, :]
                o = keep["nshift"][:, j, :]
                tj = t0[:, CT * j:CT * j + CT]
                link(nc.vector.tensor_tensor(s, t1[:, CT * j:CT * j + CT], col(f"{norm}_gamma"), ALU.mult))
                link(nc.vector.tensor_tensor(tj, s, col(f"{norm}_mean"), ALU.mult))
                link(nc.vector.tensor_tensor(o, col(f"{norm}_beta"), tj, ALU.subtract))
                if bias:
                    link(nc.vector.tensor_tensor(tj, s, col(bias), ALU.mult))
                    link(nc.vector.tensor_tensor(o, o, tj, ALU.add))
            dve.wait_ge(ident_ready, 1)
            dve.wait_ge(loaded, 16 * n_loads)
            for t in range(CT):
                for k in range(EDGE_PE):
                    nc.vector.tensor_scalar(keep["diag"][:, t, k, :], keep["ident"][:, :], keep["etaps"][:, t, k:k + 1],
                                            None, ALU.mult)
            for i in range(1, n_turned):
                take(i)


def upsample(nc, dve, small, mask, step, before):
    m32, q32, m64 = small
    n = [0]

    def link(ins):
        n[0] += 1
        ins.then_inc(step, 1)
        if n[0] < NM:
            dve.wait_ge(step, before + n[0])

    link(nc.vector.tensor_scalar(q32[:, :, :], m32[:, :, :], 0.25, None, ALU.mult))
    cols = m64[:, :, :].rearrange("p h (w a) -> p h w a", a=2)
    link(nc.vector.scalar_tensor_tensor(out=cols[:, :, 1:32, 0], in0=m32[:, :, 1:32], scalar=0.75,
                                        in1=q32[:, :, 0:31], op0=ALU.mult, op1=ALU.add))
    link(nc.vector.scalar_tensor_tensor(out=cols[:, :, 0:31, 1], in0=m32[:, :, 0:31], scalar=0.75,
                                        in1=q32[:, :, 1:32], op0=ALU.mult, op1=ALU.add))
    link(nc.vector.tensor_copy(cols[:, :, 0, 0], m32[:, :, 0]))
    link(nc.vector.tensor_copy(cols[:, :, 31, 1], m32[:, :, 31]))
    rows = mask[:, :, :].rearrange("p (h a) w -> p h a w", a=2)
    link(nc.vector.tensor_scalar(rows[:, 1:32, 0, :], m64[:, 0:31, :], 0.25, None, ALU.mult))
    link(nc.vector.tensor_scalar(rows[:, 0:31, 1, :], m64[:, 1:32, :], 0.25, None, ALU.mult))
    link(nc.vector.scalar_tensor_tensor(out=rows[:, 1:32, 0, :], in0=m64[:, 1:32, :], scalar=0.75,
                                        in1=rows[:, 1:32, 0, :], op0=ALU.mult, op1=ALU.add))
    link(nc.vector.scalar_tensor_tensor(out=rows[:, 0:31, 1, :], in0=m64[:, 0:31, :], scalar=0.75,
                                        in1=rows[:, 0:31, 1, :], op0=ALU.mult, op1=ALU.add))
    link(nc.vector.tensor_copy(rows[:, 0, 0, :], m64[:, 0, :]))
    link(nc.vector.tensor_copy(rows[:, 31, 1, :], m64[:, 31, :]))


def project_phase(nc, dram, keep, scratch):
    with ExitStack() as ctx:
        sb = lambda name, shape, dt=F32: ctx.enter_context(nc.sbuf_tensor(name, shape, dt))
        sem = lambda name: ctx.enter_context(nc.semaphore(name))
        x = [sb(f"x{p}", [P, CT, CH]) for p in range(2)]
        full = [sb(f"full{p}", [P, 4, CH]) for p in range(2)]
        high = [sb(f"high{p}", [P, 4, CH], F32R) for p in range(2)]
        low = [sb(f"low{p}", [P, 4, CH], F32R) for p in range(2)]
        v1 = [sb(f"v1{p}", [P, HEADS, NSUB, HD]) for p in range(2)]
        small = [sb("first_m32", [P, 32, 32]), sb("first_q32", [P, 32, 32]), sb("first_m64", [P, 32, WW])]
        pq = [ctx.enter_context(nc.psum_tensor(f"pq{k}", [P, CH], F32)) for k in range(4)]
        pv = [ctx.enter_context(nc.psum_tensor(f"pvp{k}", [P, 2, C], F32)) for k in range(2)]

        x_loaded = [sem(f"x_loaded{p}") for p in range(2)]
        x_used = sem("x_used")
        qk_ready = sem("qk_projected")
        v_ready = sem("v_projected")
        full_ready = sem("full_ready")
        high_ready = sem("high_ready")
        low_ready = sem("low_ready")
        v_copied = sem("v_copied")
        mask_loaded = sem("small_mask_loaded")
        mstep = sem("first_mask_step")
        qk_stored = [sem(f"qk_stored{p}") for p in range(2)]
        v_stored = [sem(f"v_stored{p}") for p in range(2)]
        block = ctx.enter_context(nc.Block())
        STEPS = B * NCH
        STORES = 6
        x_rows = dram["x"].rearrange("b (t p) h w -> p (b t) (h w)", p=P)

        q_rows = scratch["q"].rearrange("(t h c) s r n -> h s r t c n", h=2, c=NCH)
        k_rows = scratch["k"].rearrange("(t s r) n -> s r t n", s=2, r=P)


        @block.sync
        def _(sp):
            for p in range(2):
                sp.sem_inc(qk_stored[p], 16 * STORES)
                sp.sem_inc(v_stored[p], 16)

            def load(b, c, p):
                sp.dma_start(x[p][:, :, :], x_rows[:, bass.ds(b * CT, CT), bass.ds(c * CH, CH)]).then_inc(x_loaded[p], 16)

            def store(b, c, n, p):
                sp.wait_ge(high_ready, 4 * n + 4)
                sp.wait_ge(low_ready, 4 * (n + 2) + 4)
                for part, src in enumerate((high[p], low[p])):
                    for h in range(2):
                        sp.dma_start(q_rows[h, part, :, bass.ds(b * CT, CT), bass.ds(c, 1), :].rearrange("r t c n -> r t (c n)"),
                                     src[64 * h:64 * h + 64, 0:CT, :].bitcast(F32)).then_inc(qk_stored[p], 16)
                    sp.dma_start(k_rows[part, :, bass.ds(b * CT, CT), bass.ds(c * CH, CH)],
                                 src[:, CT:2 * CT, :].bitcast(F32)).then_inc(qk_stored[p], 16)
                sp.wait_ge(v_copied, 2 * (n + 1) + 2)
                sp.dma_start(scratch["v"][:, bass.ds(b * HEADS, HEADS), bass.ds(c * NSUB * HD, NSUB * HD)],
                             v1[p][:, :, :, :].rearrange("p h m d -> p h (m d)")).then_inc(v_stored[p], 16)

            load(0, 0, 0)
            load(0, 1, 1)
            sp.dma_start(small[0][:, :, :].rearrange("p h w -> p (h w)"),
                         dram["mask"].rearrange("b a h w -> (b a) (h w)")[0:1, :].broadcast_to((P, 1024))
                         ).then_inc(mask_loaded, 16)
            with sp.Fori(0, B) as b:
                with sp.Fori(0, NCH // 2 - 1) as c2:
                    for p in range(2):
                        n = b * NCH + c2 * 2 + p
                        sp.wait_ge(x_used, n + 1)
                        load(b, c2 * 2 + p + 2, p)
                        store(b, c2 * 2 + p, n, p)
                for p in range(2):
                    c = NCH - 2 + p
                    n = b * NCH + c
                    sp.wait_ge(x_used, n + 1)
                    load(B - 1, p, p)
                    store(b, c, n, p)
            for p in range(2):
                sp.wait_ge(qk_stored[p], 16 * STORES * (STEPS // 2 + 1))
                sp.wait_ge(v_stored[p], 16 * (STEPS // 2 + 1))
                sp.wait_ge(x_loaded[p], 16 * (STEPS // 2 + 1))

        @block.tensor
        def _(pe):
            with pe.Fori(0, STEPS // 2) as i2:
                for p in range(2):
                    n = i2 * 2 + p
                    pe.wait_ge(x_loaded[p], 16 * i2 + 16)
                    pe.wait_ge(full_ready, 4 * (n + 1))
                    for k in range(4):
                        w = keep["wq" if k < 2 else "wk"]
                        ot = k % 2
                        for kt in range(CT):
                            mm = nc.tensor.matmul(pq[k][:, :], w[:, kt, ot * P:(ot + 1) * P], x[p][:, kt, :],
                                                  start=(kt == 0), stop=(kt == CT - 1))
                        mm.then_inc(qk_ready, 1)
                    pe.wait_ge(v_copied, 2 * (n + 1))
                    for j in range(2):
                        for s in range(2):
                            m = 2 * j + s
                            for kt in range(CT):
                                mm = nc.tensor.matmul(pv[j][:, s, :], x[p][:, kt, m * P:(m + 1) * P],
                                                      keep["wv"][:, kt, :],
                                                      start=(s == 0 and kt == 0), stop=(kt == CT - 1),
                                                      skip_group_check=True)
                        mm.then_inc(v_ready, 1)
                        if j == 1:
                            pe.drain().then_inc(x_used, 1)

        @block.scalar
        def _(act):
            act.sem_inc(full_ready, 4)
            with act.Fori(0, STEPS // 2) as i2:
                for p in range(2):
                    n = i2 * 2 + p
                    for k in range(4):
                        act.wait_ge(low_ready, 4 * (n + 1))
                        act.wait_ge(qk_ready, 4 * n + k + 1)
                        nc.scalar.activation(full[p][:, k, :], pq[k][:, :], ACT.Identity, scale=QS if k < 2 else 1.0,
                                             bias=keep["bqs"][:, k // 2, k % 2:k % 2 + 1]).then_inc(full_ready, 1)

        @block.vector
        def _(dve):
            dve.sem_inc(v_copied, 2)
            with dve.Fori(0, STEPS // 2) as i2:
                for p in range(2):
                    n = i2 * 2 + p
                    dve.wait_ge(qk_stored[p], 16 * STORES * (i2 + 1))
                    for k in range(4):
                        dve.wait_ge(full_ready, 4 * (n + 1) + k + 1)
                        nc.vector.tensor_copy(high[p][:, k, :], full[p][:, k, :]).then_inc(high_ready, 1)
                    dve.wait_ge(v_stored[p], 16 * (i2 + 1))
                    for j in range(2):
                        dve.wait_ge(v_ready, 2 * n + j + 1)
                        for s in range(2):
                            ins = nc.vector.tensor_tensor(
                                v1[p][:, :, 2 * j + s, :], pv[j][:, s, :].rearrange("p (h d) -> p h d", h=HEADS),
                                keep["bv"][:, :].rearrange("p (h d) -> p h d", h=HEADS), ALU.add)
                        ins.then_inc(v_copied, 1)
            dve.wait_ge(mask_loaded, 16)
            upsample(nc, dve, small, keep["mask"], mstep, 0)
            dve.wait_ge(mstep, NM)

        @block.gpsimd
        def _(pool):
            pool.sem_inc(low_ready, 8)
            with pool.Fori(0, STEPS // 2) as i2:
                for p in range(2):
                    n = i2 * 2 + p
                    pool.wait_ge(qk_stored[p], 16 * STORES * (i2 + 1))
                    for k in range(4):
                        pool.wait_ge(high_ready, 4 * n + k + 1)
                        nc.gpsimd.tensor_tensor(low[p][:, k, :], full[p][:, k, :], high[p][:, k, :].bitcast(F32),
                                                ALU.subtract).then_inc(low_ready, 1)


GROUPS = [4, 4, 4, 4, 3, 3, 4, 4]
BY_VECTOR = [3]
GROUP_END = [sum(GROUPS[:k + 1]) for k in range(len(GROUPS))]
PLAIN = MT - sum(GROUPS)
QUADS = MT // 2
SUMS = (len(GROUPS) + PLAIN) // 2
BANKS = 3
TILES = 2 * MT
KV_PARTS = 4
RING = 8
ORDER = ("msmsmsmsmVmmsmssmVmsmssmmVsmssmmsmVsmsmmssmsVsmssmmsmsSsmssmmsVmssmmsVVmssmsmmsVssmmsmsVssmmmsSmmssm"
         "smVmmsssmmVmmsssmmVmmsmssmVmmsssmmSVrVsssSmsmsmsSs")
SCORES_AHEAD = 7
BLOCKS_AHEAD = 3
TAKE_NUM, TAKE_DEN, INVERT = 0, 23, 31
ADD_AFTER = [27, 33, 37]
NUM_AFTER, DEN_AFTER = 2, 7
SCALE_AFTER = 5


def adds_until(k, i):
    same = k in BY_VECTOR
    return sum(GROUPS[j] - 1 for j in range(k) if (j in BY_VECTOR) == same) + i


ADDS = {vector: sum(g - 1 for k, g in enumerate(GROUPS) if (k in BY_VECTOR) == vector) for vector in (True, False)}


def attention_phase(nc, keep, scratch):
    with ExitStack() as ctx:
        sb = lambda name, shape, dt=F32: ctx.enter_context(nc.sbuf_tensor(name, shape, dt))
        sem = lambda name: ctx.enter_context(nc.semaphore(name))
        kk = [sb(f"keys{p}", [SPLIT + 1, 2, N], F32R) for p in range(2)]
        vv = [sb(f"values{p}", [P, 2, MT, HD]) for p in range(2)]
        qq = [sb(f"queries{p}", [SPLIT + 1, 2, CH], F32R) for p in range(2)]
        prob = [sb(f"prob{r}", [P, 2, CH]) for r in range(RING)]
        psum = [sb(f"prob_sum{r}", [P, 2, CH]) for r in range(len(GROUPS))]
        ones = sb("ones", [P, HD])
        bmax = sb("block_max", [P, 2 * NSUB, MB])
        nmax = sb("negated_max", [P, 2 * NSUB], F32R)
        ident_r = sb("ident_r", [P, P], F32R)
        warm = sb("exp_warm", [P, 1])
        num_even = sb("num_even", [2 * HD, CH])
        den_even = sb("den_even", [2 * HD, CH])
        num = sb("num", [2 * HD, CH])
        den = sb("den", [2 * HD, CH])
        dcol = sb("den_col", [P, 2 * CH // P])
        rcol = sb("rec_col", [P, 2 * CH // P])
        rec = sb("rec", [2 * HD, CH])
        fuse = sb("fuse", [2 * HD, CH])
        st = [ctx.enter_context(nc.psum_tensor(f"st{i}", [P, CH], F32)) for i in range(BANKS)]
        mx = [ctx.enter_context(nc.psum_tensor(f"mx{i}", [P, CH], F32)) for i in range(BANKS)]
        acc = ctx.enter_context(nc.psum_tensor("acc", [P, CH], F32))
        dacc = ctx.enter_context(nc.psum_tensor("dacc", [P, CH], F32))

        kv_loaded = [sem(f"kv_loaded{p}") for p in range(2)]
        q_loaded = [sem(f"q_loaded{p}") for p in range(2)]
        first_keys = sem("first_head_keys_loaded")
        consts = sem("constants_ready")
        ones_row = sem("row_of_ones_ready")
        scores = sem("scores_ready")
        exp_done = sem("exp_done")
        added = {False: sem("added_by_gpsimd"), True: sem("added_by_vector")}
        v_done = sem("v_products_done")
        sums_done = sem("sum_products_done")
        mx_ready = sem("max_block_ready")
        mx_taken = sem("max_block_taken")
        nmax_ready = sem("negated_max_ready")
        mrow_ready = sem("max_row_ready")
        mrow_set = sem("max_row_set")
        num_half = sem("num_half_ready")
        den_half = sem("den_half_ready")
        num_ready = sem("num_ready")
        den_ready = sem("den_ready")
        den_stored = sem("den_stored")
        dcol_loaded = sem("den_col_loaded")
        rcol_ready = sem("rec_col_ready")
        rcol_stored = sem("rec_col_stored")
        rec_loaded = sem("rec_loaded")
        fuse_ready = sem("fuse_ready")
        fuse_stored = sem("fuse_stored")
        block = ctx.enter_context(nc.Block())

        KV_INC = 16 * 8 * KV_PARTS
        Q_INC = 16 * 6

        def add(engine, ops, u, k, i):
            own = k in BY_VECTOR
            first = GROUP_END[k] - GROUPS[k]
            if i == 1:
                engine.wait_ge(sums_done, SUMS * u + k // 2 + 1)
            else:
                engine.wait_ge(added[own], ADDS[own] * (u + 1) + adds_until(k, i - 1))
            engine.wait_ge(exp_done, TILES * (u + 1) + 2 * (first + i) + 2)
            a = prob[first % RING] if i == 1 else psum[k]
            ops.tensor_tensor(psum[k][:, :, :], a[:, :, :], prob[(first + i) % RING][:, :, :],
                              ALU.add).then_inc(added[own], 1)


        @block.sync
        def _(sp):
            sp.sem_inc(den_stored, 16)
            sp.sem_inc(fuse_stored, 16)

            def load_kv(g, p, part, parts=KV_PARTS, first=None):
                cols, vals = N // parts, MT * HD // parts
                for h in range(2):
                    for r, split in enumerate((0, 1, 0)):
                        row = (g - p + split) * P + p * 64 + h * HD
                        sp.dma_start(kk[p][r * HD:(r + 1) * HD, h, bass.ds(part * cols, cols)].bitcast(F32),
                                     scratch["k"][bass.ds(row, HD), bass.ds(part * cols, cols)]
                                     ).then_inc(first if first and h == 0 else kv_loaded[p], 16)
                    sp.dma_start(vv[p][:, h, :, :].rearrange("p m d -> p (m d)")[:, bass.ds(part * vals, vals)],
                                 scratch["v"][:, bass.ds(g * 2 + h, 1), bass.ds(part * vals, vals)]
                                 .rearrange("p a k -> p (a k)")).then_inc(kv_loaded[p], 16)

            def load_q(u, p):
                for h in range(2):
                    for r, part in enumerate((0, 0, 1)):
                        sp.dma_start(qq[p][r * HD:(r + 1) * HD, h, :].bitcast(F32),
                                     scratch["q"][bass.ds(u, 1), part, h * HD:(h + 1) * HD, :].rearrange("a r n -> (a r) n")
                                     ).then_inc(q_loaded[p], 16)

            def finish(v):
                row = scratch["den"][bass.ds(v, 1), :]
                sp.wait_ge(den_ready, v + 2)
                sp.dma_start(row.rearrange("a (h n) -> (a h) n", h=2), den[0:HD + 1:HD, :]).then_inc(den_stored, 16)
                sp.wait_ge(den_stored, 16 * (v + 2))
                sp.dma_start(dcol[:, :], row.rearrange("a (p k) -> (a p) k", p=P)).then_inc(dcol_loaded, 16)
                sp.wait_ge(rcol_ready, v + 1)
                row = scratch["rec"][bass.ds(v, 1), :]
                sp.dma_start(row.rearrange("a (p k) -> (a p) k", p=P), rcol[:, :]).then_inc(rcol_stored, 16)
                sp.wait_ge(rcol_stored, 16 * (v + 1))
                sp.wait_ge(fuse_ready, v + 1)
                for h in range(2):
                    sp.dma_start(rec[HD * h:HD * (h + 1), :], row[:, h * CH:(h + 1) * CH].broadcast_to((HD, CH))
                                 ).then_inc(rec_loaded, 16)
                sp.wait_ge(fuse_ready, v + 2)
                sp.dma_start(scratch["fuse"][bass.ds(v, 1), :, :].rearrange("a r n -> (a r) n"), fuse[:, :]
                             ).then_inc(fuse_stored, 16)

            def step(i, p):
                sp.wait_ge(scores, TILES * (i + 1))
                load_q(i + 2, p)
                finish(i)

            def steps(g, first, last):
                with sp.Fori(first, last) as c2:
                    for p in range(2):
                        step(g * NCH + c2 * 2 + p, p)

            def pair(g, p):
                with sp.Fori(0, KV_PARTS // 2) as c2:
                    for q in range(2):
                        c = c2 * 2 + q
                        sp.wait_ge(scores, TILES * (g * NCH + c + 1))
                        load_q(g * NCH + c + 2, q)
                        sp.wait_ge(v_done, QUADS * (g * NCH + 1))
                        load_kv(g + 1, p, c)
                        finish(g * NCH + c)
                steps(g, KV_PARTS // 2, NCH // 2)

            load_q(0, 0)
            load_kv(0, 0, 0, parts=1, first=first_keys)
            sp.sem_inc(kv_loaded[0], KV_INC - 16 * 5)
            load_q(1, 1)
            pair(0, 1)
            with sp.Fori(1, PAIRS // 2) as g2:
                pair(g2 * 2 - 1, 0)
                pair(g2 * 2, 1)
            steps(PAIRS - 1, 0, NCH // 2 - 1)
            finish(UNITS - 2)
            finish(UNITS - 1)
            sp.wait_ge(fuse_stored, 16 * (UNITS + 1))

        @block.tensor
        def _(pe):
            pe.sem_inc(v_done, QUADS)
            pe.sem_inc(sums_done, SUMS)

            def score(u, p, gp, i):
                pe.wait_ge(exp_done, TILES * (u + 1) + max(i - BANKS + 1, 0))
                s, h = i // 2, i % 2
                nc.tensor.matmul(st[i % BANKS][:, :], kk[gp][:, h, s * P:(s + 1) * P], qq[p][:, h, :],
                                 start=True, stop=True).then_inc(scores, 1)

            def max_block(v, p, gp, j):
                pe.wait_ge(mx_taken, MAXMM * v + j + 1)
                hn, blk = j // MB, j % MB
                h, ns = hn // NSUB, hn % NSUB
                nc.tensor.matmul(mx[j % BANKS][:, :], qq[p][0:SPLIT, h, ns * P:(ns + 1) * P],
                                 kk[gp][0:SPLIT, h, blk * CH:(blk + 1) * CH],
                                 start=True, stop=True).then_inc(mx_ready, 1)

            def max_rows(v):
                pe.wait_ge(nmax_ready, v + 1)
                for h in range(2):
                    for ns in range(NSUB):
                        i = h * NSUB + ns
                        mm = nc.tensor.matmul(mx[h][:, ns * P:(ns + 1) * P], nmax[:, i:i + 1].broadcast_to((P, P)),
                                              ident_r[:, :], start=(ns == 0), stop=True, skip_group_check=True)
                mm.then_inc(mrow_ready, 1)

            def values(u, gp, q):
                if q == 0:
                    pe.wait_ge(num_ready, u + 1)
                pe.wait_ge(exp_done, TILES * (u + 1) + 4 * q + 4)
                for a in range(2):
                    for h in range(2):
                        i = 2 * a + h
                        mm = nc.tensor.matmul(acc[HD * i:HD * (i + 1), :], vv[gp][:, h, 2 * q + a, :],
                                              prob[(2 * q + a) % RING][:, h, :], start=(q == 0), stop=(q == QUADS - 1))
                mm.then_inc(v_done, 1)

            def sums(u, i):
                if i == 0:
                    pe.wait_ge(den_ready, u + 1)
                k = 2 * i
                if k < len(GROUPS):
                    for j in (k, k + 1):
                        pe.wait_ge(added[j in BY_VECTOR], ADDS[j in BY_VECTOR] * (u + 1) + adds_until(j, GROUPS[j] - 1))
                    src = [psum[k + a] for a in range(2)]
                else:
                    t = GROUP_END[-1] + k - len(GROUPS)
                    pe.wait_ge(exp_done, TILES * (u + 1) + 2 * t + 4)
                    src = [prob[(t + a) % RING] for a in range(2)]
                for a in range(2):
                    for h in range(2):
                        n = 2 * a + h
                        mm = nc.tensor.matmul(dacc[HD * n:HD * (n + 1), :], ones[:, :], src[a][:, h, :],
                                              start=(i == 0), stop=(i == SUMS - 1))
                mm.then_inc(sums_done, 1)

            def unit(u, p, gp, ahead, after):
                done = {"s": SCORES_AHEAD, "m": BLOCKS_AHEAD, "V": 0, "S": 0, "r": 0}
                for op in ORDER:
                    n = done[op]
                    done[op] += 1
                    if op == "V":
                        values(u, gp, n)
                    elif op == "S":
                        sums(u, n)
                    elif op == "s" and n < TILES:
                        score(u, p, gp, n)
                    elif op == "s" and ahead:
                        if n == TILES:
                            pe.wait_ge(mrow_set, 2 * (u + 1) + 2)
                        score(u + 1, 1 - p, ahead[0], n - TILES)
                    elif op == "r" and ahead:
                        max_rows(u + 1)
                    elif op == "m":
                        v, q, keys, first = (u + 1, 1 - p, ahead, 0) if n < MAXMM else (u + 2, p, after, MAXMM)
                        if keys:
                            if n == first:
                                for w, value in keys[1]:
                                    pe.wait_ge(w, value)
                            max_block(v, q, keys[0], n - first)

            def pair(g2, gp, more):
                g = g2 * 2 + gp
                same = lambda c2, d: (gp, [(q_loaded[d % 2], Q_INC * (g * (NCH // 2) + c2 + d // 2 + 1))])
                nk = (kv_loaded[1 - gp], KV_INC * (g2 + 1 + gp))
                other = lambda c2, d: (1 - gp, same(c2, d)[1] + [nk]) if more else None
                with pe.Fori(0, NCH // 2 - 1) as c2:
                    unit(g * NCH + c2 * 2, 0, gp, same(c2, 1), same(c2, 2))
                    unit(g * NCH + c2 * 2 + 1, 1, gp, same(c2, 2), same(c2, 3))
                c2 = NCH // 2 - 1
                unit(g * NCH + c2 * 2, 0, gp, same(c2, 1), other(c2, 2))
                unit(g * NCH + c2 * 2 + 1, 1, gp, other(c2, 2), other(c2, 3))

            pe.wait_ge(consts, 2)
            pe.wait_ge(q_loaded[0], Q_INC)
            pe.wait_ge(first_keys, 16 * 3)
            for j in range(MAXMM):
                if j == MAXMM // 2:
                    pe.wait_ge(kv_loaded[0], KV_INC)
                max_block(0, 0, 0, j)
            max_rows(0)
            pe.wait_ge(mrow_set, 2)
            pe.wait_ge(ones_row, 2)
            for i in range(SCORES_AHEAD):
                score(0, 0, 0, i)
            if BLOCKS_AHEAD:
                pe.wait_ge(q_loaded[1], Q_INC)
            for j in range(BLOCKS_AHEAD):
                max_block(1, 1, 0, j)
            with pe.Fori(0, PAIRS // 2 - 1) as g2:
                pair(g2, 0, True)
                pair(g2, 1, True)
            pair(PAIRS // 2 - 1, 0, True)
            pair(PAIRS // 2 - 1, 1, False)

        @block.scalar
        def _(act):
            def rows(v, p):
                act.wait_ge(mrow_ready, v + 1)
                nc.scalar.copy(qq[p][SPLIT:SPLIT + 1, 0, :], mx[0][SPLIT:SPLIT + 1, :]).then_inc(mrow_set, 1)

            def num_half_out(v):
                act.wait_ge(num_ready, v + 1)
                act.wait_ge(v_done, QUADS * (v + 2))
                nc.scalar.copy(num_even[:, :], acc[0:2 * HD, :]).then_inc(num_half, 1)

            def den_half_out(v):
                act.wait_ge(den_ready, v + 1)
                act.wait_ge(sums_done, SUMS * (v + 2))
                nc.scalar.copy(den_even[:, :], dacc[0:2 * HD, :]).then_inc(den_half, 1)

            def buffer_free(u, s):
                v, t = (u + 1, s - RING) if s >= RING else (u, s - RING + MT)
                act.wait_ge(v_done, QUADS * v + t // 2 + 1)
                if t < GROUP_END[-1]:
                    k = sum(e <= t for e in GROUP_END)
                    own = k in BY_VECTOR
                    i = max(t - GROUP_END[k] + GROUPS[k], 1)
                    act.wait_ge(added[own], ADDS[own] * v + adds_until(k, i))
                else:
                    act.wait_ge(sums_done, SUMS * v + (len(GROUPS) + t - GROUP_END[-1]) // 2 + 1)

            def unit(u, p, prev=True, ahead=True):
                for i in range(TILES):
                    s, h = i // 2, i % 2
                    act.wait_ge(scores, TILES * u + i + 1)
                    if h == 0:
                        buffer_free(u, s)
                    nc.scalar.activation(prob[s % RING][:, h, :], st[i % BANKS][:, :], ACT.Exp).then_inc(exp_done, 1)
                    if prev and i == NUM_AFTER:
                        num_half_out(u - 1)
                    if prev and i == DEN_AFTER:
                        den_half_out(u - 1)
                if ahead:
                    rows(u + 1, 1 - p)

            act.sem_inc(exp_done, TILES)
            act.wait_ge(consts, 2)
            nc.scalar.activation(warm[:, :], ones[:, 0:1], ACT.Exp)
            rows(0, 0)
            unit(0, 0, prev=False)
            with act.Fori(0, UNITS // 2 - 1) as u2:
                unit(u2 * 2 + 1, 1)
                unit(u2 * 2 + 2, 0)
            unit(UNITS - 1, 1, ahead=False)
            num_half_out(UNITS - 1)
            den_half_out(UNITS - 1)

        @block.vector
        def _(dve):
            dve.sem_inc(mx_taken, BANKS)
            dve.sem_inc(added[True], ADDS[True])
            dve.sem_inc(num_ready, 1)
            dve.sem_inc(den_ready, 1)

            def take_num(v):
                dve.wait_ge(num_half, v + 1)
                dve.wait_ge(fuse_ready, v + 1)
                nc.vector.tensor_tensor(num[:, :], acc[2 * HD:4 * HD, :], num_even[:, :], ALU.add).then_inc(num_ready, 1)

            def take_den(v):
                dve.wait_ge(den_half, v + 1)
                dve.wait_ge(den_stored, 16 * (v + 1))
                nc.vector.tensor_tensor(den[:, :], dacc[2 * HD:4 * HD, :], den_even[:, :], ALU.add).then_inc(den_ready, 1)

            def invert(v):
                dve.wait_ge(dcol_loaded, 16 * (v + 1))
                nc.vector.reciprocal(rcol[:, :], dcol[:, :]).then_inc(rcol_ready, 1)

            additions = [(k, i) for k in BY_VECTOR for i in range(1, GROUPS[k])]

            def between(v, j, prev=True, older=True):
                if older:
                    if j == TAKE_NUM:
                        take_num(v - 2)
                    if j == TAKE_DEN:
                        take_den(v - 2)
                    if j == INVERT:
                        invert(v - 2)
                for at, (k, i) in zip(ADD_AFTER, additions):
                    if prev and j == at:
                        add(dve, nc.vector, v - 1, k, i)

            def maxima(v, p, prev=True, older=True):
                for j in range(MAXMM):
                    dve.wait_ge(mx_ready, MAXMM * v + j + 1)
                    nc.vector.tensor_reduce(bmax[:, j // MB, j % MB:j % MB + 1], mx[j % BANKS][:, :], AX.X,
                                            ALU.max).then_inc(mx_taken, 1)
                    between(v, j, prev, older)
                dve.wait_ge(mx_taken, MAXMM * v + MAXMM + BANKS)
                nc.vector.tensor_reduce(nmax[:, :], bmax[:, :, :], AX.X, ALU.max, negate=True).then_inc(nmax_ready, 1)
                dve.wait_ge(mrow_ready, v + 1)
                nc.vector.tensor_copy(qq[p][SPLIT:SPLIT + 1, 1, :], mx[1][SPLIT:SPLIT + 1, :]).then_inc(mrow_set, 1)

            nc.vector.memset(ones[:, :], 1.0).then_inc(consts, 1)
            nc.vector.tensor_copy(ident_r[:, :], keep["ident"][:, :]).then_inc(consts, 1)
            maxima(0, 0, prev=False, older=False)
            maxima(1, 1, older=False)
            with dve.Fori(1, UNITS // 2) as v2:
                maxima(v2 * 2, 0)
                maxima(v2 * 2 + 1, 1)
            for j in range(MAXMM):
                between(UNITS, j)
            take_num(UNITS - 1)
            take_den(UNITS - 1)
            invert(UNITS - 1)

        @block.gpsimd
        def _(pool):
            pool.sem_inc(added[False], ADDS[False])
            pool.sem_inc(fuse_ready, 1)
            for p in range(2):
                nc.gpsimd.memset(kk[p][SPLIT:SPLIT + 1, :, :].bitcast(F32), 1.0).then_inc(ones_row, 1)

            def scale(v):
                pool.wait_ge(num_ready, v + 2)
                pool.wait_ge(rec_loaded, 32 * (v + 1))
                pool.wait_ge(fuse_stored, 16 * (v + 1))
                nc.gpsimd.tensor_tensor(fuse[:, :], num[:, :], rec[:, :], ALU.mult).then_inc(fuse_ready, 1)

            def unit(u, prev=True):
                for k, size in enumerate(GROUPS):
                    if k not in BY_VECTOR:
                        for i in range(1, size):
                            add(pool, nc.gpsimd, u, k, i)
                    if k == SCALE_AFTER and prev:
                        scale(u - 1)

            unit(0, prev=False)
            with pool.Fori(1, UNITS) as u:
                unit(u)
            scale(UNITS - 1)


EDGE_PE = 2
SHARED = 3
EDGE_DVE = TAPS - EDGE_PE - SHARED
DEFORM_DVE = TAPS - SHARED
ADDED = SHARED * CT


def image_phase(nc, dram, keep, scratch, out):
    with ExitStack() as ctx:
        sb = lambda name, shape, dt=F32: ctx.enter_context(nc.sbuf_tensor(name, shape, dt))
        sem = lambda name: ctx.enter_context(nc.semaphore(name))
        xf = [sb(f"xf{p}", [P, 2 * CT, CH]) for p in range(2)]
        mask = keep["mask"]
        small = [sb("m32", [P, 32, 32]), sb("q32", [P, 32, 32]), sb("m64", [P, 32, WW])]
        diff = sb("diff", [P, CT, CH])
        y = sb("y", [P, CT, PR, PW])
        o1 = sb("o1", [P, CT, PR, PW])
        edge = sb("edge", [P, CT, N])
        conv = [sb(f"conv{p}", [P, CT, CH]) for p in range(2)]
        tap = sb("weighted_pixels", [P, ADDED, CH])
        ypart = sb("ypart", [P, CT, NCH])
        ysum = sb("ysum", [P, CT])
        hid = sb("hid", [HID, 1])
        nexp = sb("nexp", [P, CT])
        gate1 = sb("gate1", [P, CT])
        gate = sb("gate", [P, CT])
        fus = sb("fus", [P, CT, C])
        last = [sb(f"last{p}", [P, CT, CH]) for p in range(2)]
        front = [[ctx.enter_context(nc.psum_tensor(f"front{p}{t}", [P, CH], F32)) for t in range(CT)] for p in range(2)]
        back = [[ctx.enter_context(nc.psum_tensor(f"back{p}{t}", [P, CH], F32)) for t in range(CT)] for p in range(2)]

        mask_loaded = sem("mask_loaded")
        mstep = sem("mask_step")
        xf_loaded = [sem(f"xf_loaded{p}") for p in range(2)]
        borders = sem("borders_zeroed")
        hybrid = sem("hybrid_ready")
        diffed = sem("diff_ready")
        masked = sem("masked_ready")
        y_ready = sem("y_ready")
        part_ready = sem("partial_sum_ready")
        sum_ready = sem("sum_ready")
        hid_mm = sem("hidden_product")
        hid_ready = sem("hidden_ready")
        z_ready = sem("gate_product")
        nexp_ready = sem("gate_exp")
        gstep = sem("gate_step")
        edge_mm = sem("edge_product")
        edge_step = sem("edge_step")
        tap_ready = sem("weighted_pixels_ready")
        tap_added = sem("weighted_pixels_added")
        edge_ready = sem("edge_ready")
        fus_mm = sem("fusion_product")
        o1_ready = sem("o1_ready")
        deform_step = sem("deform_step")
        bal_mm = sem("balance_product")
        last_ready = sem("last_ready")
        res_ready = sem("result_ready")
        stored = [sem(f"stored{p}") for p in range(2)]
        block = ctx.enter_context(nc.Block())

        XF_INC = 16 * (1 + HEADS // 2)
        HALF = NCH // 2
        x_rows = dram["x"].rearrange("b (t p) h w -> p (b t) (h w)", p=P)
        out_rows = out.rearrange("b (t p) h w -> p (b t) (h w)", p=P)

        EARLIER = 2 * CT
        freed = lambda n: EARLIER + CT * (n - 1)
        tile_done = lambda n, t: EARLIER + CT * n + t + 1
        edge_round = lambda b, c: 2 * NCH * b + c
        deform_round = lambda b, c: 2 * NCH * b + NCH + c
        added_in = lambda r, i: ADDED * (r + 1) + i + 1

        def inner(t, ot, c, rows=ROWS, k=4):
            return t[:, ot, bass.ds(c * ROWS + k // 3, rows), k % 3:k % 3 + WW]

        as_rows = lambda ap: ap.rearrange("p (r w) -> p r w", w=WW)

        @block.sync
        def _(sp):
            sp.sem_inc(mask_loaded, 16)
            for p in range(2):
                sp.sem_inc(stored[p], 16)

            def load_mask(b):
                sp.dma_start(small[0][:, :, :].rearrange("p h w -> p (h w)"),
                             dram["mask"].rearrange("b a h w -> (b a) (h w)")[bass.ds(b, 1), :].broadcast_to((P, 1024))
                             ).then_inc(mask_loaded, 16)

            def load(b, c, p):
                sp.dma_start(xf[p][:, 0:CT, :], x_rows[:, bass.ds(b * CT, CT), bass.ds(c * CH, CH)]
                             ).then_inc(xf_loaded[p], 16)
                for g in range(HEADS // 2):
                    sp.dma_start(xf[p][64 * (g % 2):64 * (g % 2) + 64, CT + g // 2, :],
                                 scratch["fuse"][bass.ds((b * (HEADS // 2) + g) * NCH + c, 1), :, :]
                                 .rearrange("a r n -> (a r) n")).then_inc(xf_loaded[p], 16)

            def load_next(b, c, p):
                sp.wait_ge(y_ready, tile_done(b * NCH + c, CT - 1))
                load(b, c + 2, p)

            def store(b, first, last_c):
                with sp.Fori(first // 2, last_c // 2) as c2:
                    for p in range(2):
                        c = c2 * 2 + p
                        sp.wait_ge(res_ready, CT * (b * NCH + c) + CT)
                        sp.dma_start(out_rows[:, bass.ds(b * CT, CT), bass.ds(c * CH, CH)], last[p][:, :, :]
                                     ).then_inc(stored[p], 16)

            def image(b, more):
                with sp.Fori(1, HALF - 1) as c2:
                    for p in range(2):
                        load_next(b, c2 * 2 + p, p)
                if more:
                    sp.wait_ge(mstep, NM * (b + 1))
                    load_mask(b + 1)
                    for p in range(2):
                        sp.wait_ge(y_ready, tile_done(b * NCH + NCH - 2 + p, CT - 1))
                        load(b + 1, p, p)
                store(b, 0, NCH // 2)
                if more:
                    for p in range(2):
                        load_next(b + 1, p, p)
                store(b, NCH // 2, NCH)

            for p in range(2):
                load(0, p, p)
            for p in range(2):
                load_next(0, p, p)
            with sp.Fori(0, B - 1) as b:
                image(b, True)
            image(B - 1, False)
            for p in range(2):
                sp.wait_ge(stored[p], 16 * (B * HALF + 1))

        @block.tensor
        def _(pe):
            def mix(b, c, p, c2):
                n = b * NCH + c
                pe.wait_ge(xf_loaded[p], XF_INC * (b * HALF + c2 + 1))
                pe.wait_ge(diffed, freed(n))
                for ot in range(CT):
                    for kt in range(2 * CT):
                        mm = nc.tensor.matmul(front[p][ot][:, :], keep["wf"][:, kt, ot * P:(ot + 1) * P],
                                              xf[p][:, kt, :], start=(kt == 0), stop=(kt == 2 * CT - 1))
                    mm.then_inc(hybrid, 1)

            def edges(b, c, p, nxt=1):
                n = b * NCH + c
                pe.wait_ge(y_ready, tile_done(n + nxt, CT - 1))
                pe.wait_ge(edge_step, EARLIER * EDGE_DVE + CT * EDGE_DVE * (n - 2) + CT)
                pe.wait_ge(last_ready, EARLIER + CT * NCH * b)
                for ct in range(CT):
                    for k in range(EDGE_PE):
                        mm = nc.tensor.matmul(as_rows(back[p][ct][:, :]), keep["diag"][:, ct, k, :],
                                              inner(y, ct, c, k=k), start=(k == 0), stop=(k == EDGE_PE - 1))
                    mm.then_inc(edge_mm, 1)

            def fuse(b, c, p):
                n = b * NCH + c
                pe.wait_ge(o1_ready, freed(n))
                pe.wait_ge(edge_ready, tile_done(n, CT - 1))
                for ot in range(CT):
                    for kt in range(CT):
                        nc.tensor.matmul(front[p][ot][:, :], keep["fu"][:, CT + kt, ot * P:(ot + 1) * P],
                                         edge[:, kt, bass.ds(c * CH, CH)], start=(kt == 0), stop=False)
                pe.wait_ge(gstep, 4 * b + 4)
                for ot in range(CT):
                    for kt in range(CT):
                        mm = nc.tensor.matmul(as_rows(front[p][ot][:, :]), fus[:, kt, ot * P:(ot + 1) * P],
                                              inner(y, kt, c), start=False, stop=(kt == CT - 1))
                    mm.then_inc(fus_mm, 1)

            def balance(b, c, p):
                n = b * NCH + c
                pe.wait_ge(last_ready, freed(n))
                pe.wait_ge(tap_added, added_in(deform_round(b, c), ADDED - 1))
                for ot in range(CT):
                    for kt in range(CT):
                        mm = nc.tensor.matmul(back[p][ot][:, :], keep["ba"][:, kt, ot * P:(ot + 1) * P],
                                              conv[p][:, kt, :], start=(kt == 0), stop=(kt == CT - 1))
                    mm.then_inc(bal_mm, 1)

            pe.sem_inc(bal_mm, EARLIER)
            pe.wait_ge(borders, 8)
            def image(b, more):
                with pe.Fori(0, HALF - 1) as c2:
                    for p in range(2):
                        mix(b, c2 * 2 + p + 2, p, c2 + 1)
                        edges(b, c2 * 2 + p, p)
                edges(b, NCH - 2, 0)
                pe.wait_ge(sum_ready, b + 1)
                for kt in range(CT):
                    mm = nc.tensor.matmul(front[1][0][0:HID, 0:1], keep["fc1"][:, kt, :], ysum[:, kt:kt + 1],
                                          start=(kt == 0), stop=(kt == CT - 1))
                mm.then_inc(hid_mm, 1)
                pe.wait_ge(hid_ready, b + 1)
                for ot in range(CT):
                    mm = nc.tensor.matmul(front[1][1][:, ot:ot + 1], keep["fc2"][:, ot * P:(ot + 1) * P], hid[:, :],
                                          start=(ot == 0), stop=True, skip_group_check=True)
                mm.then_inc(z_ready, 1)
                edges(b, NCH - 1, 1, nxt=0)
                for c in range(3):
                    fuse(b, c, c % 2)
                fuse(b, 3, 1)
                balance(b, 0, 0)
                with pe.Fori(0, HALF - 2) as c2:
                    for p in range(2):
                        fuse(b, c2 * 2 + p + 4, p)
                        balance(b, c2 * 2 + p + 1, 1 - p)
                if more:
                    for p in range(2):
                        pe.wait_ge(o1_ready, tile_done(b * NCH + NCH - 2 + p, CT - 1))
                        mix(b + 1, p, p, 0)
                for c in range(NCH - 3, NCH):
                    balance(b, c, c % 2)

            for p in range(2):
                mix(0, p, p, 0)
            with pe.Fori(0, B - 1) as b:
                image(b, True)
            image(B - 1, False)

        @block.scalar
        def _(act):
            def weigh(src, weights, b, c, r):
                for i in range(SHARED):
                    for ct in range(CT):
                        k = TAPS - SHARED + i
                        j = i * CT + ct
                        act.wait_ge(tap_added, added_in(r - 1, j))
                        nc.scalar.activation(as_rows(tap[:, j, :]), inner(src, ct, c, k=k), ACT.Identity,
                                             scale=keep[weights][:, ct, k:k + 1]).then_inc(tap_ready, 1)

            def weigh_y(b, c, nxt=1):
                act.wait_ge(y_ready, tile_done(b * NCH + c + nxt, CT - 1))
                weigh(y, "etaps", b, c, edge_round(b, c))

            def relu(b, c, p):
                for ct in range(CT):
                    act.wait_ge(tap_added, added_in(edge_round(b, c), ADDED - CT + ct))
                    nc.scalar.activation(edge[:, ct, bass.ds(c * CH, CH)], conv[p][:, ct, :], ACT.Relu,
                                         scale=keep["nscale"][:, 0, ct:ct + 1],
                                         bias=keep["nshift"][:, 0, ct:ct + 1]).then_inc(edge_ready, 1)

            def fused(b, c, p):
                n = b * NCH + c
                for ot in range(CT):
                    act.wait_ge(fus_mm, CT * n + ot + 1)
                    nc.scalar.activation(inner(o1, ot, c), as_rows(front[p][ot][:, :]), ACT.Identity,
                                         scale=keep["nscale"][:, 1, ot:ot + 1],
                                         bias=keep["nshift"][:, 1, ot:ot + 1]).then_inc(o1_ready, 1)

            def weigh_o1(b, c, nxt=1):
                act.wait_ge(o1_ready, tile_done(b * NCH + c + nxt, CT - 1))
                weigh(o1, "dtaps", b, c, deform_round(b, c))

            def balanced(b, c, p, c2):
                n = b * NCH + c
                act.wait_ge(stored[p], 16 * (b * HALF + c2 + 1))
                for ot in range(CT):
                    act.wait_ge(bal_mm, tile_done(n, ot))
                    nc.scalar.activation(last[p][:, ot, :], back[p][ot][:, :], ACT.Identity,
                                         scale=keep["nscale"][:, 2, ot:ot + 1],
                                         bias=keep["nshift"][:, 2, ot:ot + 1]).then_inc(last_ready, 1)

            for s in (edge_ready, o1_ready, last_ready):
                act.sem_inc(s, EARLIER)
            with act.Fori(0, B) as b:
                weigh_y(b, 0)
                with act.Fori(0, HALF - 2) as c2:
                    for p in range(2):
                        weigh_y(b, c2 * 2 + p + 1)
                        relu(b, c2 * 2 + p, p)
                weigh_y(b, NCH - 3)
                relu(b, NCH - 4, 0)
                act.wait_ge(hid_mm, b + 1)
                nc.scalar.activation(hid[:, :], front[1][0][0:HID, 0:1], ACT.Relu, scale=1.0 / N).then_inc(hid_ready, 1)
                act.wait_ge(z_ready, b + 1)
                nc.scalar.activation(nexp[:, :], front[1][1][:, 0:CT], ACT.Exp, scale=-1.0).then_inc(nexp_ready, 1)
                weigh_y(b, NCH - 2)
                relu(b, NCH - 3, 1)
                weigh_y(b, NCH - 1, nxt=0)
                relu(b, NCH - 2, 0)
                fused(b, 0, 0)
                relu(b, NCH - 1, 1)
                fused(b, 1, 1)
                weigh_o1(b, 0)
                fused(b, 2, 0)
                weigh_o1(b, 1)
                with act.Fori(0, HALF - 2) as c2:
                    for p in range(2):
                        fused(b, c2 * 2 + p + 3, 1 - p)
                        weigh_o1(b, c2 * 2 + p + 2)
                        balanced(b, c2 * 2 + p, p, c2)
                fused(b, NCH - 1, 1)
                weigh_o1(b, NCH - 2)
                balanced(b, NCH - 4, 0, HALF - 2)
                weigh_o1(b, NCH - 1, nxt=0)
                for c in range(NCH - 3, NCH):
                    balanced(b, c, c % 2, c // 2)

        @block.gpsimd
        def _(pool):
            def add_taps(r, p, step, before):
                for j in range(ADDED):
                    ct = j % CT
                    if j < CT:
                        pool.wait_ge(step, before + ct + 1)
                    else:
                        pool.wait_ge(tap_added, added_in(r, j - CT))
                    pool.wait_ge(tap_ready, ADDED * r + j + 1)
                    nc.gpsimd.tensor_tensor(conv[p][:, ct, :], conv[p][:, ct, :], tap[:, j, :], ALU.add
                                            ).then_inc(tap_added, 1)

            pool.sem_inc(tap_added, ADDED)
            for t in (y, o1):
                for edge_rows in (t[:, :, 0, :], t[:, :, PR - 1, :], t[:, :, 1:PR - 1, 0], t[:, :, 1:PR - 1, PW - 1]):
                    nc.gpsimd.memset(edge_rows, 0.0).then_inc(borders, 1)
            with pool.Fori(0, B) as b:
                with pool.Fori(0, HALF) as c2:
                    for p in range(2):
                        c = c2 * 2 + p
                        add_taps(edge_round(b, c), p, edge_step,
                                 EARLIER * EDGE_DVE + CT * EDGE_DVE * (b * NCH + c) + CT * (EDGE_DVE - 1))
                with pool.Fori(0, HALF) as c2:
                    for p in range(2):
                        c = c2 * 2 + p
                        add_taps(deform_round(b, c), p, deform_step,
                                 CT * DEFORM_DVE * (b * NCH + c) + CT * (DEFORM_DVE - 1))

        @block.vector
        def _(dve):
            def make_y(b, c, p):
                n = b * NCH + c
                for ot in range(CT):
                    dve.wait_ge(hybrid, CT * n + ot + 1)
                    dve.wait_ge(y_ready, tile_done(n - 1, ot))
                    nc.vector.scalar_tensor_tensor(
                        out=diff[:, ot, :], in0=front[p][ot][:, :],
                        scalar=keep["vec"][:, VEC.index("bf"), ot:ot + 1], in1=xf[p][:, ot, :],
                        op0=ALU.add, op1=ALU.subtract).then_inc(diffed, 1)
                for ot in range(CT):
                    dve.wait_ge(diffed, tile_done(n, ot))
                    dve.wait_ge(mstep, NM * b + NM)
                    nc.vector.tensor_tensor(as_rows(diff[:, ot, :]), as_rows(diff[:, ot, :]),
                                            mask[:, bass.ds(c * ROWS, ROWS), :], ALU.mult).then_inc(masked, 1)
                for ot in range(CT):
                    dve.wait_ge(masked, CT * n + ot + 1)
                    nc.vector.tensor_tensor(inner(y, ot, c), as_rows(diff[:, ot, :]),
                                            as_rows(xf[p][:, ot, :]), ALU.add).then_inc(y_ready, 1)
                for ot in range(CT):
                    dve.wait_ge(y_ready, tile_done(n, ot))
                    nc.vector.tensor_reduce(ypart[:, ot, bass.ds(c, 1)], inner(y, ot, c), AX.XY,
                                            ALU.add).then_inc(part_ready, 1)

            def edges(b, c, p):
                n = b * NCH + c
                dve.wait_ge(edge_ready, freed(n))
                dve.wait_ge(bal_mm, EARLIER + CT * NCH * b)
                base = EDGE_DVE * (EARLIER + CT * n)
                for i in range(EDGE_DVE):
                    for ct in range(CT):
                        k = EDGE_PE + i
                        if i == 0:
                            dve.wait_ge(edge_mm, CT * n + ct + 1)
                        else:
                            dve.wait_ge(edge_step, base + CT * (i - 1) + ct + 1)
                        nc.vector.scalar_tensor_tensor(
                            out=as_rows(conv[p][:, ct, :]), in0=inner(y, ct, c, k=k),
                            scalar=keep["etaps"][:, ct, k:k + 1],
                            in1=as_rows(back[p][ct][:, :] if i == 0 else conv[p][:, ct, :]),
                            op0=ALU.mult, op1=ALU.add).then_inc(edge_step, 1)

            def means(b):
                dve.wait_ge(part_ready, CT * NCH * (b + 1))
                nc.vector.tensor_reduce(ysum[:, :], ypart[:, :, :], AX.X, ALU.add).then_inc(sum_ready, 1)

            def gated(b):
                dve.wait_ge(nexp_ready, b + 1)
                nc.vector.tensor_scalar(gate1[:, :], nexp[:, :], 1.0, None, ALU.add).then_inc(gstep, 1)
                dve.wait_ge(gstep, 4 * b + 1)
                nc.vector.reciprocal(gate[:, :], gate1[:, :]).then_inc(gstep, 1)
                dve.wait_ge(gstep, 4 * b + 2)
                for kt in range(CT):
                    nc.vector.tensor_scalar(fus[:, kt, :], keep["fu"][:, kt, :], gate[:, kt:kt + 1], None,
                                            ALU.mult).then_inc(gstep, 1)

            def deform(b, c, p, nxt=1):
                n = b * NCH + c
                dve.wait_ge(o1_ready, tile_done(n + nxt, CT - 1))
                dve.wait_ge(edge_ready, tile_done(b * NCH + NCH - 2 + p, CT - 1))
                dve.wait_ge(bal_mm, freed(n))
                base = CT * DEFORM_DVE * n
                for k in range(DEFORM_DVE):
                    for ct in range(CT):
                        dst = as_rows(conv[p][:, ct, :])
                        src = inner(o1, ct, c, k=k)
                        w = keep["dtaps"][:, ct, k:k + 1]
                        if k == 0:
                            ins = nc.vector.tensor_scalar(dst, src, w, None, ALU.mult)
                        else:
                            dve.wait_ge(deform_step, base + CT * (k - 1) + ct + 1)
                            ins = nc.vector.scalar_tensor_tensor(out=dst, in0=src, scalar=w, in1=dst,
                                                                 op0=ALU.mult, op1=ALU.add)
                        ins.then_inc(deform_step, 1)

            def result(b, c, p):
                for ot in range(CT):
                    dve.wait_ge(last_ready, tile_done(b * NCH + c, ot))
                    nc.vector.tensor_tensor(as_rows(last[p][:, ot, :]), as_rows(last[p][:, ot, :]),
                                            inner(y, ot, c), ALU.mult).then_inc(res_ready, 1)

            def image(b, more):
                with dve.Fori(0, HALF - 2) as c2:
                    for p in range(2):
                        make_y(b, c2 * 2 + p + 2, p)
                        edges(b, c2 * 2 + p, p)
                make_y(b, NCH - 2, 0)
                edges(b, NCH - 4, 0)
                make_y(b, NCH - 1, 1)
                means(b)
                edges(b, NCH - 3, 1)
                gated(b)
                edges(b, NCH - 2, 0)
                edges(b, NCH - 1, 1)
                for p in range(2):
                    deform(b, p, p)
                deform(b, 2, 0)
                with dve.Fori(0, HALF - 2) as c2:
                    for p in range(2):
                        deform(b, c2 * 2 + p + 3, 1 - p)
                        result(b, c2 * 2 + p, p)
                if more:
                    dve.wait_ge(mask_loaded, 16 * (b + 1) + 16)
                    upsample(nc, dve, small, keep["mask"], mstep, NM * (b + 1))
                deform(b, NCH - 1, 1, nxt=0)
                if more:
                    for p in range(2):
                        make_y(b + 1, p, p)
                for c in range(NCH - 4, NCH):
                    result(b, c, c % 2)

            dve.sem_inc(y_ready, EARLIER)
            dve.sem_inc(diffed, EARLIER)
            dve.sem_inc(edge_step, EARLIER * EDGE_DVE)
            dve.sem_inc(mstep, NM)
            dve.wait_ge(borders, 8)
            for p in range(2):
                make_y(0, p, p)
            with dve.Fori(0, B - 1) as b:
                image(b, True)
            image(B - 1, False)


def build(nc, dram, out):
    with ExitStack() as ctx:
        sb = lambda name, shape: ctx.enter_context(nc.sbuf_tensor(name, shape, F32))
        keep = {
            "ident": sb("ident", [P, P]),
            "vec": sb("vec", [P, NVEC, CT]),
            "bqs": sb("bqs", [P, 2, CT]),
            "bv": sb("bv_rows", [P, C]),
            "nscale": sb("nscale", [P, 3, CT]),
            "nshift": sb("nshift", [P, 3, CT]),
            "mask": sb("mask", [P, HH, WW]),
            "etaps": sb("etaps", [P, CT, TAPS]),
            "dtaps": sb("dtaps", [P, CT, TAPS]),
            "diag": sb("diag", [P, CT, EDGE_PE, P]),
            "fc1": sb("fc1T", [P, CT, HID]),
            "fc2": sb("fc2T", [HID, C]),
        }
        for w, ots, kts in WEIGHTS:
            keep[w] = sb(f"{w}T", [P, kts, ots * P])
        scratch = {
            "q": nc.dram_tensor("q_scratch", [UNITS, 2, 64, CH], F32).ap(),
            "k": nc.dram_tensor("k_scratch", [PAIRS * 2 * 64, N], F32).ap(),
            "v": nc.dram_tensor("v_scratch", [P, B * HEADS, MT * HD], F32).ap(),
            "den": nc.dram_tensor("den_scratch", [UNITS, 2 * CH], F32).ap(),
            "rec": nc.dram_tensor("rec_scratch", [UNITS, 2 * CH], F32).ap(),
            "fuse": nc.dram_tensor("fuse_scratch", [UNITS, 2 * HD, CH], F32).ap(),
        }
        setup_phase(nc, dram, keep)
        project_phase(nc, dram, keep, scratch)
        attention_phase(nc, keep, scratch)
        image_phase(nc, dram, keep, scratch, out)


_INS = {
    "x": "x", "mask": "L0_conv_mask", "wq": "L0_conv_Wq", "bq": "L0_conv_bq", "wk": "L0_conv_Wk", "bk": "L0_conv_bk",
    "wv": "L0_conv_Wv", "bv": "L0_conv_bv", "wf": "L0_conv_Wf", "bf": "L0_conv_bf",
    "edge_w": "L1_conv_edge_w", "edge_gamma": "L1_conv_edge_gamma", "edge_beta": "L1_conv_edge_beta",
    "edge_mean": "L1_conv_edge_mean", "edge_var": "L1_conv_edge_var", "fc1": "L1_conv_fc1_w", "fc2": "L1_conv_fc2_w",
    "fu": "L1_conv_fusion_w", "fusion_b": "L1_conv_fusion_b", "bn1_gamma": "L1_conv_bn1_gamma",
    "bn1_beta": "L1_conv_bn1_beta", "bn1_mean": "L1_conv_bn1_mean", "bn1_var": "L1_conv_bn1_var",
    "deform_w": "L1_conv_deform_w", "ba": "L1_conv_balance_w", "balance_b": "L1_conv_balance_b",
    "bn2_gamma": "L1_conv_bn2_gamma", "bn2_beta": "L1_conv_bn2_beta", "bn2_mean": "L1_conv_bn2_mean",
    "bn2_var": "L1_conv_bn2_var",
}


def kernel(**inputs):
    import numpy as _np
    import concourse.bacc as _bacc
    from concourse import mybir as _mybir
    from concourse.bass_utils import run_bass_kernel_spmd as _run

    nc = _bacc.Bacc("TRN2", target_bir_lowering=False, num_devices=1)
    arrays, dram = {}, {}
    for short, name in _INS.items():
        a = _np.ascontiguousarray(inputs[name])
        arrays[f"in_{name}"] = a
        dram[short] = nc.dram_tensor(f"in_{name}", a.shape, _mybir.dt.from_np(a.dtype), kind="ExternalInput").ap()
    out = nc.dram_tensor("out_dram", (B, C, HH, WW), F32, kind="ExternalOutput").ap()
    build(nc, dram, out)
    r = _run(nc, [arrays], core_ids=[0])
    return r.results[0]["out_dram"]
```
